# Optimizing a Trainium2 kernel written in Bass

```python
import numpy as np
import jax
import jax.numpy as jnp

def _softmax(x, axis=-1):
    return jax.nn.softmax(x, axis=axis)

def _gelu(x):
    return jax.nn.gelu(x, approximate=True)

def _silu(x):
    return jax.nn.silu(x)

def _sigmoid(x):
    return jax.nn.sigmoid(x)

def _layernorm(x, axis=-1, eps=1e-05):
    m = jnp.mean(x, axis=axis, keepdims=True)
    v = jnp.var(x, axis=axis, keepdims=True)
    return (x - m) / jnp.sqrt(v + eps)

def _scatter_add(tgt, idx, src, axis=0):
    return tgt.at[idx].add(src)

def _segment_sum(src, seg, n):
    return jax.ops.segment_sum(src, seg, n)
kernel_name = 'mk_adj_preln_d4_adj_r2_753952'

def setup_inputs(seed: int=0):
    np.random.seed(seed)
    _w = jnp.asarray

    def _rec_inputs():
        import jax
        import jax.numpy as jnp
        _gk = jax.random.key(seed)
        x = -0.0002928 + 1 * jax.random.normal(jax.random.fold_in(_gk, 1), (1354, 256), jnp.float32)
        _w = (1.0 + jnp.arange(1354, dtype=jnp.float32)) ** (-0.5)
        _w = _w / _w.mean()
        _pij = jnp.clip(0.00590842 * _w[:, None] * _w[None, :], 0.0, 1.0)
        _a = jax.random.uniform(jax.random.fold_in(_gk, 2), (1354, 1354)) < _pij
        _a = jnp.logical_or(_a, jnp.swapaxes(_a, -1, -2))
        _a = jnp.logical_or(_a, jnp.eye(1354, dtype=bool))
        _af = _a.astype(jnp.float32)
        _af = _af * jax.random.uniform(jax.random.fold_in(_gk, 3), (1354, 1354), jnp.float32, 0.05, 5.41998)
        adj = _af
        return (x, adj)
    x, adj = _rec_inputs()

    def _L0_gnn_setup():
        import jax, jax.numpy as jnp
        import numpy as np
        N = 4096
        D = 256
        key = jax.random.key(seed)
        ks = jax.random.split(key, 6)
        s = 1.0 / np.sqrt(D)
        return {'x': jax.random.normal(ks[0], (N, D), jnp.float32), 'spatial_encoding': jax.random.normal(ks[1], (N, N), jnp.float32), 'edge_encoding': jax.random.normal(ks[2], (N, N), jnp.float32), 'Wq': jax.random.normal(ks[3], (D, D), jnp.float32) * s, 'bq': jnp.zeros((D,), jnp.float32), 'Wk': jax.random.normal(ks[4], (D, D), jnp.float32) * s, 'bk': jnp.zeros((D,), jnp.float32), 'Wv': jax.random.normal(ks[5], (D, D), jnp.float32) * s, 'bv': jnp.zeros((D,), jnp.float32)}
    _L0_gnn_all = _L0_gnn_setup()
    _L0_gnn_in = {k: v for k, v in _L0_gnn_all.items() if k in ('Wq', 'bq', 'Wk', 'bk', 'Wv', 'bv')}
    del _L0_gnn_all

    def _L1_gnn_setup():
        import jax, jax.numpy as jnp
        import numpy as np
        N = 3072
        D_IN = 256
        D_OUT = 256
        DENSITY = 0.005
        key = jax.random.key(seed)
        ks = jax.random.split(key, 12)
        x = jax.random.normal(ks[0], (N, D_IN), dtype=jnp.float32)
        adj_a = (jax.random.uniform(ks[1], (N, N)) < DENSITY).astype(jnp.float32)
        adj_b = (jax.random.uniform(ks[2], (N, N)) < DENSITY).astype(jnp.float32)
        W_sa = jax.random.normal(ks[3], (D_IN, D_OUT), dtype=jnp.float32) * (1.414 / np.sqrt(D_IN + D_OUT))
        a_sa = jax.random.normal(ks[4], (1, 2 * D_OUT), dtype=jnp.float32) * (1.414 / np.sqrt(1 + 2 * D_OUT))
        stdv = 1.0 / np.sqrt(D_OUT)
        W_gcnb = jax.random.uniform(ks[5], (D_IN, D_OUT), minval=-stdv, maxval=stdv, dtype=jnp.float32)
        b_gcnb = jax.random.uniform(ks[6], (D_OUT,), minval=-stdv, maxval=stdv, dtype=jnp.float32)
        s = 1.0 / np.sqrt(2 * D_IN)
        Wa = jax.random.uniform(ks[7], (1, 2 * D_IN), minval=-s, maxval=s, dtype=jnp.float32)
        ba = jax.random.uniform(ks[8], (1,), minval=-s, maxval=s, dtype=jnp.float32)
        Wb = jax.random.uniform(ks[9], (1, 2 * D_IN), minval=-s, maxval=s, dtype=jnp.float32)
        bb = jax.random.uniform(ks[10], (1,), minval=-s, maxval=s, dtype=jnp.float32)
        return {'x': x, 'adj_a': adj_a, 'adj_b': adj_b, 'W_sa': W_sa, 'a_sa': a_sa, 'W_gcnb': W_gcnb, 'b_gcnb': b_gcnb, 'Wa': Wa, 'ba': ba, 'Wb': Wb, 'bb': bb}
    _L1_gnn_all = _L1_gnn_setup()
    _L1_gnn_in = {k: v for k, v in _L1_gnn_all.items() if k in ('W_sa', 'a_sa', 'W_gcnb', 'b_gcnb', 'Wa', 'ba', 'Wb', 'bb')}
    del _L1_gnn_all

    def _L2_gnn_setup():
        import jax, jax.numpy as jnp
        import numpy as np
        N = 4096
        F_IN = 256
        F_OUT = 256
        DENSITY = 0.01
        key = jax.random.key(seed)
        k_x, k_adj, k_w, k_b = jax.random.split(key, 4)
        input_features = jax.random.normal(k_x, (N, F_IN), dtype=jnp.float32)
        adj = (jax.random.uniform(k_adj, (N, N)) < DENSITY).astype(jnp.float32)
        idx = jnp.arange(N)
        adj = adj.at[idx, idx].set(1.0)
        W = jax.random.normal(k_w, (F_IN, F_OUT), dtype=jnp.float32) / np.sqrt(F_IN)
        b = jax.random.normal(k_b, (F_OUT,), dtype=jnp.float32) * 0.01
        return {'input_features': input_features, 'adj': adj, 'W': W, 'b': b}
    _L2_gnn_all = _L2_gnn_setup()
    _L2_gnn_in = {k: v for k, v in _L2_gnn_all.items() if k in ('W', 'b')}
    del _L2_gnn_all

    def _L3_gnn_setup():
        import jax, jax.numpy as jnp
        import numpy as np
        N = 4096
        D_IN = 256
        D_OUT = 256
        EDGE_P = 0.004

        def _xavier_uniform(key, fan_in, fan_out):
            bound = np.sqrt(6.0 / (fan_in + fan_out))
            return jax.random.uniform(key, (fan_in, fan_out), jnp.float32, -bound, bound)
        key = jax.random.key(seed)
        kx, ks, kw, ku = jax.random.split(key, 4)
        x = jax.random.normal(kx, (N, D_IN), dtype=jnp.float32)
        S = (jax.random.uniform(ks, (N, N), dtype=jnp.float32) < EDGE_P).astype(jnp.float32)
        W = _xavier_uniform(kw, D_IN, D_OUT)
        U = _xavier_uniform(ku, D_OUT, D_OUT)
        return {'x': x, 'S': S, 'W': W, 'U': U}
    _L3_gnn_all = _L3_gnn_setup()
    _L3_gnn_in = {k: v for k, v in _L3_gnn_all.items() if k in ('W', 'U')}
    del _L3_gnn_all
    return {'x': x, 'adj': adj, 'L0_gnn_Wq': _L0_gnn_in['Wq'], 'L0_gnn_bq': _L0_gnn_in['bq'], 'L0_gnn_Wk': _L0_gnn_in['Wk'], 'L0_gnn_bk': _L0_gnn_in['bk'], 'L0_gnn_Wv': _L0_gnn_in['Wv'], 'L0_gnn_bv': _L0_gnn_in['bv'], 'L1_gnn_W_sa': _L1_gnn_in['W_sa'], 'L1_gnn_a_sa': _L1_gnn_in['a_sa'], 'L1_gnn_W_gcnb': _L1_gnn_in['W_gcnb'], 'L1_gnn_b_gcnb': _L1_gnn_in['b_gcnb'], 'L1_gnn_Wa': _L1_gnn_in['Wa'], 'L1_gnn_ba': _L1_gnn_in['ba'], 'L1_gnn_Wb': _L1_gnn_in['Wb'], 'L1_gnn_bb': _L1_gnn_in['bb'], 'L2_gnn_W': _L2_gnn_in['W'], 'L2_gnn_b': _L2_gnn_in['b'], 'L3_gnn_W': _L3_gnn_in['W'], 'L3_gnn_U': _L3_gnn_in['U']}

def reference(x, adj, L0_gnn_Wq, L0_gnn_bq, L0_gnn_Wk, L0_gnn_bk, L0_gnn_Wv, L0_gnn_bv, L1_gnn_W_sa, L1_gnn_a_sa, L1_gnn_W_gcnb, L1_gnn_b_gcnb, L1_gnn_Wa, L1_gnn_ba, L1_gnn_Wb, L1_gnn_bb, L2_gnn_W, L2_gnn_b, L3_gnn_W, L3_gnn_U):
    import jax
    import jax.numpy as jnp

    def _L0_gnn_ref(x, spatial_encoding, edge_encoding, Wq, bq, Wk, bk, Wv, bv):
        import jax, jax.numpy as jnp
        import numpy as np
        N = 4096
        D = 256
        q = x @ Wq.T + bq
        k = x @ Wk.T + bk
        v = x @ Wv.T + bv
        scale = 1.0 / jnp.sqrt(jnp.asarray(q.shape[-1], q.dtype))
        a = q @ k.T * scale + spatial_encoding + edge_encoding
        attn = jax.nn.softmax(a, axis=-1)
        return attn @ v

    def _L1_gnn_ref(x, adj_a, adj_b, W_sa, a_sa, W_gcnb, b_gcnb, Wa, ba, Wb, bb):
        import jax, jax.numpy as jnp
        import numpy as np
        N = 3072
        D_IN = 256
        D_OUT = 256
        DENSITY = 0.005
        type_sum_a = adj_a @ x
        type_sum_b = adj_b @ x
        attn_a = jax.nn.sigmoid(jnp.concatenate([type_sum_a, x], axis=1) @ Wa.T + ba)
        attn_b = jax.nn.sigmoid(jnp.concatenate([type_sum_b, x], axis=1) @ Wb.T + bb)
        h = x @ W_sa
        Hd = h.shape[1]
        s_left = h @ a_sa[0, :Hd]
        s_right = h @ a_sa[0, Hd:]
        scores = s_left[:, None] + s_right[None, :]
        e = jnp.where(adj_a != 0, jnp.exp(-jax.nn.leaky_relu(scores, 0.01)), 0.0)
        attn = e / (jnp.sum(e, axis=1, keepdims=True) + 1e-05)
        x_a = attn @ h
        x_b = adj_b @ (x @ W_gcnb) + b_gcnb
        return jax.nn.sigmoid(attn_a * x_a + attn_b * x_b)

    def _L2_gnn_ref(input_features, adj, W, b):
        import jax, jax.numpy as jnp
        import numpy as np
        N = 4096
        F_IN = 256
        F_OUT = 256
        DENSITY = 0.01
        A = (adj != 0).astype(input_features.dtype)
        hidden = input_features @ W + b
        deg = jnp.sum(A, axis=0)
        return A @ hidden / deg[:, None]

    def _L3_gnn_ref(x, S, W, U):
        import jax, jax.numpy as jnp
        import numpy as np
        N = 4096
        D_IN = 256
        D_OUT = 256
        EDGE_P = 0.004

        def _xavier_uniform(key, fan_in, fan_out):
            bound = np.sqrt(6.0 / (fan_in + fan_out))
            return jax.random.uniform(key, (fan_in, fan_out), jnp.float32, -bound, bound)
        n = x.shape[0]
        S = S + jnp.eye(n, dtype=S.dtype)
        h = x @ W
        scores = h @ U @ h.T
        mask = S > 0
        scores = jnp.where(mask, scores, -jnp.inf)
        att = jax.nn.softmax(scores, axis=-1)
        att = att * mask.astype(att.dtype)
        S_tilde = S * att
        return S_tilde @ h
    h = jnp.maximum(_layernorm(x, axis=-1), 0.0)
    x = x + _L0_gnn_ref(h, adj, adj, L0_gnn_Wq, L0_gnn_bq, L0_gnn_Wk, L0_gnn_bk, L0_gnn_Wv, L0_gnn_bv)
    h = jnp.maximum(_layernorm(x, axis=-1), 0.0)
    x = x + _L1_gnn_ref(h, adj, adj, L1_gnn_W_sa, L1_gnn_a_sa, L1_gnn_W_gcnb, L1_gnn_b_gcnb, L1_gnn_Wa, L1_gnn_ba, L1_gnn_Wb, L1_gnn_bb)
    h = jnp.maximum(_layernorm(x, axis=-1), 0.0)
    x = x + _L2_gnn_ref(h, adj, L2_gnn_W, L2_gnn_b)
    h = jnp.maximum(_layernorm(x, axis=-1), 0.0)
    x = x + _L3_gnn_ref(h, adj, L3_gnn_W, L3_gnn_U)
    return x

_drawn_inputs = setup_inputs


def setup_inputs(seed=0):
    import zlib

    import numpy as np

    out = dict(_drawn_inputs(seed))
    spreads = {'L0_gnn_bq': (0.0, 0.366), 'L0_gnn_bk': (0.0, 2.0), 'L0_gnn_bv': (0.0, 0.1)}
    factors = {'L1_gnn_W_sa': 25.886, 'L1_gnn_a_sa': 39.995, 'L1_gnn_b_gcnb': 48.038, 'L2_gnn_b': 4.396}
    for name, (base, spread) in spreads.items():
        noise = np.random.default_rng([zlib.crc32(name.encode()), seed]).standard_normal(out[name].shape)
        drawn = base * np.exp(spread * noise) if base else spread * noise
        out[name] = jnp.asarray(drawn.astype(out[name].dtype))
    for name, factor in factors.items():
        out[name] = (out[name] * factor).astype(out[name].dtype)
    return out
```

```python
from contextlib import ExitStack

import concourse.bass as bass
from concourse import mybir

ALU = mybir.AluOpType
ACT = mybir.ActivationFunctionType
F32 = mybir.dt.float32
F32R = mybir.dt.float32r
AX_X = mybir.AxisListType.X

P = 128
N = 1354
D = 256
C = D // P
NB = -(-N // P)
NP = NB * P
LAST = N - (NB - 1) * P
W = D + 2
WA = D + 4
BANK = 512
SCORE_CHUNKS = [(0, 452), (452, 452), (904, N - 904)]
PAIRS = (NB + 1) // 2
XB = 3
PER_BANK = 4
X_PARTS = [(0, 3), (3, 7), (7, NB - 1)]
EPS = 1e-5
BIG = 3.0e38
TINY = 2.0 ** -60
HALF_SCALE = 0.5 * D ** -0.5


def graph_layers_kernel(nc, x, adj, adjT, wq, wk, wvT, wsa, wgcn, w2, w3, w3T, u3T, asa, cols, rows, eye, out):
    with ExitStack() as ctx:
        def sb(name, shape, dt=F32):
            return ctx.enter_context(nc.sbuf_tensor(name, shape, dt))

        def ps(name, shape):
            return ctx.enter_context(nc.psum_tensor(name, shape, F32))

        def sem(name):
            return ctx.enter_context(nc.semaphore(name))

        def f(ap):
            return ap.bitcast(F32)

        def tiles(ap):
            return ap.rearrange("p (t m) -> p t m", m=P)

        x_sb = sb("x_sb", [P, NB, D])
        adjT_sb = sb("adjT_sb", [P, NB, NB * P])
        hT_hi = sb("hT_hi", [P, NB * W], F32R)
        hT_lo = sb("hT_lo", [P, NB * W], F32R)
        v_hi = sb("v_hi", [P, NB, W], F32R)
        v_lo = sb("v_lo", [P, NB, W], F32R)
        wa_hi = sb("wa_hi", [P, C, WA], F32R)
        wa_lo = sb("wa_lo", [P, C, WA], F32R)
        wb_hi = sb("wb_hi", [P, C, W], F32R)
        wb_lo = sb("wb_lo", [P, C, W], F32R)
        wl_hi = sb("wl_hi", [P, C, P], F32R)
        wl_lo = sb("wl_lo", [P, C, P], F32R)
        wv_sb = sb("wv_sb", [P, C, W])
        wsa_sb = sb("wsa_sb", [P, C, WA])
        wg_sb = sb("wg_sb", [P, C, W])
        gram = sb("gram", [P, C, D])
        wl_sb = sb("wl_sb", [P, C, P])
        asa_sb = sb("asa_sb", [P, 2, D])
        rows_sb = sb("rows_sb", [P, 3 * D + 2])
        cols_sb = sb("cols_sb", [P, 6, C])
        wlr = sb("wlr", [P, C, 2])
        bqk = sb("bqk", [P, C])
        bqc = sb("bqc", [P, 1])
        bq_rep = sb("bq_rep", [P, C, P])
        ident = sb("ident", [P, P])
        a_buf = [sb(f"a_buf{u}", [P, NP]) for u in range(2)]
        m_buf = [sb(f"m_buf{u}", [P, NP], F32R) for u in range(2)]
        s_buf = sb("s_buf", [P, NP])
        p_buf = sb("p_buf", [P, NP])
        pt_hi = sb("pt_hi", [P, NP], F32R)
        pt_lo = sb("pt_lo", [P, NP], F32R)
        at_hi = sb("at_hi", [P, NP], F32R)
        at_lo = sb("at_lo", [P, NP], F32R)
        h_hi = sb("h_hi", [P, 3, C, P], F32R)
        h_lo = sb("h_lo", [P, 3, C, P], F32R)
        z_buf = sb("z_buf", [P, 2, D])
        t2_buf = sb("t2_buf", [P, D])
        th_buf = sb("th_buf", [P, D])
        vb_buf = sb("vb_buf", [P, 2, D])
        stats = sb("stats", [P, 6])
        mv = sb("mv", [P, 2])
        veps = sb("veps", [P, 1])
        mv_all = sb("mv_all", [P, NB, 2])
        veps_all = sb("veps_all", [P, NB])
        mhalf = sb("mhalf", [P, 1])
        mean_all = sb("mean_all", [P, NB])
        rstd_all = sb("rstd_all", [P, NB])
        right_all = sb("right_all", [P, NB])
        ext_all = sb("ext_all", [P, NB, 2])
        ones = sb("ones", [P, 1])
        r_all = sb("r_all", [P, NB])
        mx3 = sb("mx3", [P, 4])
        mx = sb("mx", [P, 1])
        mr = sb("mr", [P, 1])
        nb = sb("nb", [P, 1])
        rowsum = sb("rowsum", [P, 2])
        rinv = sb("rinv", [P, 1])
        zz = sb("zz", [P, 2])
        zzb = sb("zzb", [P, 2])
        ez = sb("ez", [P, 2])
        al = sb("al", [P, 2])
        den = sb("den", [P, 1])
        rden = sb("rden", [P, 1])
        deg = sb("deg", [P, NB])
        rdeg = sb("rdeg", [P, NB])

        hT = [t[:, 0:C * NP].rearrange("p (c n) -> p c n", c=C) for t in (hT_hi, hT_lo)]
        g = [t[:, :].rearrange("p (b w) -> p b w", w=W) for t in (hT_hi, hT_lo)]
        slb, sums_buf = a_buf

        def h_block(i, layer):
            if layer in (0, 3):
                return [t[:, :, i * P:(i + 1) * P] for t in hT]
            return [t[:, i % 3, :, :] for t in (h_hi, h_lo)]

        m_tmp, cnt = m_buf
        w2_sb, w3_sb = wv_sb[:, :, 0:D], wg_sb[:, :, 0:D]
        t_hi, t_lo = [h[:, 0:2, :, :].rearrange("p a c n -> p (a c n)").rearrange("p (c n) -> p c n", c=C)
                      for h in (h_hi, h_lo)]
        t1_buf = vb_buf[:, 0, :]
        wq_sb, wk_sb = [p_buf[:, n * C * D:(n + 1) * C * D].rearrange("p (c n) -> p c n", c=C) for n in range(2)]
        w3T_sb, u3T_sb = [s_buf[:, n * C * D:(n + 1) * C * D].rearrange("p (c n) -> p c n", c=C) for n in range(2)]
        bv_row, b2_row, bg_row, bab = rows_sb[:, 0:D], rows_sb[:, D:2 * D], rows_sb[:, 2 * D:3 * D], rows_sb[:, 3 * D:]
        bq_col, bk_col = cols_sb[:, 0, :], cols_sb[:, 1, :]

        ps_s = ps("ps_s", [P, 3, BANK])
        ps_x = ps("ps_x", [P, XB, BANK])
        ps_o = ps("ps_o", [P, BANK])
        ps_t = ps("ps_t", [P, BANK])
        ps_pair = [ps_o, ps_t]
        ps_left = [ps_s[:, 2, :], ps_x[:, 2, :]]

        x_in = [sem(f"x_in{part}") for part in range(len(X_PARTS))]
        w_in, v_in, lw_in, adjT_in = (sem(n) for n in ("w_in", "v_in", "lw_in", "adjT_in"))
        w2_in, w3_in = sem("w2_in"), sem("w3_in")
        adj_in = [sem("adj_in0"), sem("adj_in1")]
        out_sent = sem("out_sent")
        passed = sem("passed")
        consts_set, pads_set, ident_in = sem("consts_set"), sem("pads_set"), sem("ident_in")
        prep_mm, prep_cp, prep_v = sem("prep_mm"), sem("prep_cp"), sem("prep_v")
        w_hi_set, w_lo_set = sem("w_hi_set"), sem("w_lo_set")
        stats_done, mv_done, veps_set, ln_done = sem("stats_done"), sem("mv_done"), sem("veps_set"), sem("ln_done")
        z_done, zt_done, hhi_done, hlo_done = sem("z_done"), sem("zt_done"), sem("hhi_done"), sem("hlo_done")
        proj_done, biased = sem("proj_done"), sem("biased")
        vhi_done, vlo_done = sem("vhi_done"), sem("vlo_done")
        t_done, thi_done, tlo_done = sem("t_done"), sem("thi_done"), sem("tlo_done")
        scored, added, maxed, shifted, nb_done = (sem("scored"), sem("added"), sem("maxed"), sem("shifted"),
                                                  sem("nb_done"))
        exp_done, p_done, pt_done = sem("exp_done"), sem("p_done"), sem("pt_done")
        phi_done, plo_done, agg_done = sem("phi_done"), sem("plo_done"), sem("agg_done")
        hi_used, hi1_used, ahi_used = sem("hi_used"), sem("hi1_used"), sem("ahi_used")
        rinv_done, x_added = sem("rinv_done"), sem("x_added")
        eye_added, mask3_done = sem("eye_added"), sem("mask3_done")
        sums_done, masked_done, leaky_done, exp1_done = (sem("sums_done"), sem("masked_done"), sem("leaky_done"),
                                                         sem("exp1_done"))
        nonzero_done, deg_mm = sem("nonzero_done"), sem("deg_mm")
        phi1_done, plo1_done, ahi_done, alo_done = sem("phi1_done"), sem("plo1_done"), sem("ahi_done"), sem("alo_done")
        xa_done, xb_done, t1_done = sem("xa_done"), sem("xb_done"), sem("t1_done")
        den_set, rden_done, zz_done, t2_done, ez_done = (sem("den_set"), sem("rden_done"), sem("zz_done"),
                                                         sem("t2_done"), sem("ez_done"))
        al_step, z1_done, th_done, half_done, counted = (sem("al_step"), sem("z1_done"), sem("th_done"),
                                                         sem("half_done"), sem("counted"))
        x1_added, deg_done, mask2_done, agg2_done, x2_added = (sem("x1_added"), sem("deg_done"), sem("mask2_done"),
                                                               sem("agg2_done"), sem("x2_added"))

        from_one = [agg_done, proj_done, x1_added, agg2_done, ln_done, mv_done, th_done, vlo_done, x_added, hlo_done,
                    t1_done, t2_done, zz_done, hi_used, hi1_used, ahi_used,
                    plo_done]

        def start_counts(eng, *sems):
            for s in sems:
                eng.sem_inc(s, 1)

        def wait(eng, s, value):
            if not (isinstance(value, int) and value <= 0):
                eng.wait_ge(s, value + 1 if any(s is t for t in from_one) else value)

        def wait_apart(eng, s, value):
            wait(eng, s, value)
            if not isinstance(value, int):
                eng.sem_inc(passed, 1)

        def pairs(eng, count, step):
            with eng.Fori(0, count // 2, 1) as k:
                for u in range(2):
                    step(2 * k + u, u, k)
            if count % 2:
                step(count - 1, 0, count // 2)

        def products(eng, out_ap, lhs, rhs, first, last, skip=False):
            eng.matmul(out_ap, lhs[0], rhs[0], start=first, stop=False, skip_group_check=skip)
            eng.matmul(out_ap, lhs[0], rhs[1], start=False, stop=False, skip_group_check=skip)
            return eng.matmul(out_ap, lhs[1], rhs[0], start=False, stop=last, skip_group_check=skip)

        block = ctx.enter_context(nc.Block())

        @block.sync
        def _(sp):
            for part, (b0, b1) in enumerate(X_PARTS):
                sp.dma_start(x_sb[:, b0:b1, :],
                             x[b0 * P:b1 * P, :].rearrange("(b p) d -> p b d", p=P)).then_inc(x_in[part], 16)
            sp.wait_ge(pads_set, 1)
            sp.dma_start(x_sb[0:LAST, NB - 1, :], x[(NB - 1) * P:N, :]).then_inc(x_in[-1], 16)
            for dst, src in ((wq_sb, wq), (wk_sb, wk)):
                sp.dma_start(dst[:, :, :], src.rearrange("(c p) n -> p c n", p=P)).then_inc(w_in, 16)
            sp.dma_start(wv_sb[:, :, 0:D], wvT.rearrange("(c p) n -> p c n", p=P)).then_inc(w_in, 16)
            sp.dma_start(cols_sb[:, :, :], cols).then_inc(v_in, 16)
            sp.dma_start(rows_sb[:, :], rows.partition_broadcast(P)).then_inc(v_in, 16)
            sp.dma_start(asa_sb[:, :, :], asa.partition_broadcast(P)).then_inc(v_in, 16)
            sp.dma_start(ident[:, :], eye).then_inc(ident_in, 16)

            def adj_rows(i, u, half, a):
                base = 6 * a if u == 0 else 5 * a
                if a == 0:
                    if not isinstance(i, int) or i >= 2:
                        wait_apart(sp, added, 3 * i - 3)
                        wait_apart(sp, nonzero_done, i - 1)
                elif not isinstance(i, int) or i >= 2:
                    wait(sp, p_done, i - 1)
                sp.dma_start(a_buf[u][:, 0:N], adj[bass.ds(i * P, P), :]).then_inc(adj_in[u], 16)

            def adj_last(a):
                if a == 0:
                    wait(sp, added, 3 * (NB - 2))
                    wait(sp, nonzero_done, NB - 2)
                else:
                    wait(sp, p_done, NB - 2)
                sp.dma_start(a_buf[0][0:LAST, 0:N], adj[(NB - 1) * P:N, :]).then_inc(adj_in[0], 16)

            adj_rows(0, 0, 0, 0)
            adj_rows(1, 1, 0, 0)
            for dst, src in ((w3T_sb, w3T), (u3T_sb, u3T)):
                sp.dma_start(dst[:, :, :], src.rearrange("(c p) n -> p c n", p=P)).then_inc(lw_in, 16)
            for dst, src in ((wsa_sb, wsa), (wg_sb, wgcn)):
                sp.dma_start(dst[:, :, 0:D], src.rearrange("(c p) n -> p c n", p=P)).then_inc(lw_in, 16)
            with sp.Fori(1, (NB - 1) // 2, 1) as k:
                for u in range(2):
                    adj_rows(2 * k + u, u, k, 0)
            adj_last(0)
            sp.dma_start(adjT_sb[:, :, :], adjT.rearrange("b p n -> p b n")).then_inc(adjT_in, 16)
            sp.wait_ge(w_lo_set, 2)
            sp.dma_start(w2_sb, w2.rearrange("(c p) n -> p c n", p=P)).then_inc(w2_in, 16)
            sp.wait_ge(w_lo_set, 5)
            sp.dma_start(w3_sb, w3.rearrange("(c p) n -> p c n", p=P)).then_inc(w3_in, 16)
            sp.wait_ge(masked_done, NB)
            adj_rows(0, 0, 0, 1)
            adj_rows(1, 1, 0, 1)
            with sp.Fori(1, (NB - 1) // 2, 1) as k:
                for u in range(2):
                    adj_rows(2 * k + u, u, k, 1)
            adj_last(1)

            def send(i):
                wait(sp, x_added, NB + i + 1)
                sp.dma_start(out[bass.ds(i * P, P), :], x_sb[:, i, :]).then_inc(out_sent, 16)

            with sp.Fori(0, NB - 1, 1) as i:
                send(i)
            wait(sp, x_added, 2 * NB)
            sp.dma_start(out[(NB - 1) * P:N, :], x_sb[0:LAST, NB - 1, :]).then_inc(out_sent, 16)
            sp.wait_ge(out_sent, 16 * NB)

        @block.gpsimd
        def _(pool):
            pool.memset(x_sb[64:P, NB - 1, :], 0.0).then_inc(pads_set, 1)
            pool.wait_ge(pads_set, 1)
            pool.memset(mhalf[:, :], -0.5)
            pool.memset(p_buf[:, N:NP], 0.0).then_inc(consts_set, 1)
            pool.wait_ge(consts_set, 1)

            def ln(i, base):
                wait_apart(pool, mv_done, base + i + 1)
                pool.tensor_scalar(veps[:, :], mv[:, 1:2], EPS, None, ALU.add).then_inc(veps_set, 1)
                pool.tensor_copy(mean_all[:, bass.ds(i, 1)], mv[:, 0:1])
                wait(pool, veps_set, len(X_PARTS) + base - NB + i + 1)
                pool.tensor_tensor(rstd_all[:, bass.ds(i, 1)], veps[:, :], mhalf[:, :], ALU.pow).then_inc(ln_done, 1)

            start_counts(pool, ln_done, x1_added)
            for part, (b0, b1) in enumerate(X_PARTS):
                b1 = NB if part == len(X_PARTS) - 1 else b1
                wait(pool, mv_done, b1)
                pool.tensor_scalar(veps_all[:, b0:b1], mv_all[:, b0:b1, 1], EPS, None, ALU.add).then_inc(veps_set, 1)
                pool.tensor_copy(mean_all[:, b0:b1], mv_all[:, b0:b1, 0])
                pool.wait_ge(veps_set, part + 1)
                pool.tensor_tensor(rstd_all[:, b0:b1], veps_all[:, b0:b1], mhalf[:, 0:1].broadcast_to((P, b1 - b0)),
                                   ALU.pow).then_inc(ln_done, b1 - b0)

            def count(i, rows):
                wait(pool, counted, i + 1)
                wait(pool, nonzero_done, i + 1)
                pool.tensor_tensor(cnt[0:rows, 0:N], f(cnt[0:rows, 0:N]), f(m_tmp[0:rows, 0:N]),
                                   ALU.add).then_inc(counted, 1)

            pool.memset(f(cnt[:, :]), 0.0).then_inc(counted, 1)
            count(0, P)
            with pool.Fori(0, NB - 2, 1) as i:
                count(i + 1, P)
                ln(i, NB)
            count(NB - 1, LAST)
            pool.wait_ge(counted, NB + 1)
            for i in range(NB - 2, NB):
                ln(i, NB)
            wait(pool, vlo_done, 3 * NB)

            def sums(i):
                wait(pool, masked_done, i)
                pool.tensor_tensor(tiles(sums_buf[:, :]),
                                   slb[:, bass.ds(i * P, P)].unsqueeze(1).broadcast_to((P, NB, P)),
                                   right_all[:, :].unsqueeze(2).broadcast_to((P, NB, P)),
                                   ALU.add).then_inc(sums_done, 1)

            def adj_lo(i):
                wait(pool, xb_done, i)
                wait(pool, ahi_done, i + 1)
                pool.tensor_tensor(at_lo[:, :], adjT_sb[:, i, :], f(at_hi[:, :]), ALU.subtract).then_inc(alo_done, 1)

            def half(i):
                wait_apart(pool, th_done, i + 1)
                pool.tensor_scalar(th_buf[:, :], th_buf[:, :], 0.5, 0.5, ALU.mult, ALU.add).then_inc(half_done, 1)
                wait(pool, half_done, i + 1)
                pool.tensor_tensor(x_sb[:, i, :], x_sb[:, i, :], th_buf[:, :], ALU.add).then_inc(x1_added, 1)

            sums(0)
            sums(1)
            adj_lo(0)
            sums(2)
            with pool.Fori(0, NB - 3, 1) as i:
                adj_lo(i + 1)
                sums(i + 3)
                half(i)
                ln(i, 2 * NB)
            for i in range(NB - 3, NB):
                if i + 1 < NB:
                    adj_lo(i + 1)
                half(i)
                ln(i, 2 * NB)
            with pool.Fori(0, NB, 1) as i:
                ln(i, 3 * NB)

            def plus_eye(i, u, half_i):
                wait(pool, adj_in[u], 16 * (half_i + 1 + (6 if u == 0 else 5)))
                pool.tensor_tensor(a_buf[u][:, bass.ds(i * P, P)], a_buf[u][:, bass.ds(i * P, P)], ident[:, :],
                                   ALU.add).then_inc(eye_added, 1)

            def times_s(i, u):
                wait(pool, exp_done, NB + i + 1)
                pool.tensor_tensor(p_buf[:, 0:N], p_buf[:, 0:N], a_buf[u][:, 0:N], ALU.mult).then_inc(p_done, 1)

            plus_eye(0, 0, 0)
            plus_eye(1, 1, 0)
            with pool.Fori(0, (NB - 3) // 2, 1) as k:
                for u in range(2):
                    times_s(2 * k + u, u)
                    plus_eye(2 * k + u + 2, u, k + 1)
            times_s(NB - 3, 0)
            pool.wait_ge(adj_in[0], 16 * ((NB - 1) // 2 + 1 + 6))
            pool.tensor_tensor(a_buf[0][:, (NB - 1) * P:N], a_buf[0][:, (NB - 1) * P:N], ident[:, 0:LAST],
                               ALU.add).then_inc(eye_added, 1)
            times_s(NB - 2, 1)
            times_s(NB - 1, 0)

        @block.scalar
        def _(act):
            start_counts(act, th_done, t1_done)

            def split_w(dst, src, n):
                act.activation(dst, src, ACT.Copy).then_inc(w_hi_set, 1)

            def h_hi_part(i, layer):
                wait(act, zt_done, layer * NB + i + 1)
                if layer in (1, 2) and i >= 3:
                    wait(act, proj_done, layer * NB + i - 2)
                act.activation(h_block(i, layer)[0], ps_x[:, i % 2, 0:D].rearrange("p (c n) -> p c n", c=C),
                               ACT.Relu).then_inc(hhi_done, 1)

            def values(i, layer):
                u = i % 2
                if layer in (0, 2):
                    wait(act, biased, (NB if layer else 0) + i + 1)
                    act.activation(v_hi[:, i, 0:D], vb_buf[:, u, :], ACT.Copy).then_inc(vhi_done, 1)
                else:
                    wait(act, proj_done, layer * NB + i + 1)
                    if layer == 1:
                        act.activation(slb[:, i * P:(i + 1) * P], ps_left[u][:, 0:P], ACT.Copy, scale=TINY)
                        act.activation(g[0][:, i, :], ps_pair[u][:, 0:W], ACT.Copy).then_inc(vhi_done, 1)
                    act.activation(v_hi[:, i, 0:D], ps_s[:, u, 0:D], ACT.Copy).then_inc(vhi_done, 1)

            def project_all(layer):
                h_hi_part(0, layer)
                h_hi_part(1, layer)
                for i in range(NB + 1):
                    if i >= 1:
                        values(i - 1, layer)
                    if i + 2 < NB:
                        h_hi_part(i + 2, layer)

            def t_hi_part(pair, n, a):
                wait(act, t_done, a * PAIRS + pair + 1)
                for c in range(C):
                    src = ps_t[:, c * D:c * D + n]
                    if a == 0:
                        ins = act.activation(t_hi[:, c, 0:n], src, ACT.Identity, bias=bqk[:, c:c + 1])
                    else:
                        ins = act.activation(t_hi[:, c, 0:n], src, ACT.Copy)
                ins.then_inc(thi_done, 1)

            def exp(i, u, a):
                wait(act, nb_done, a * NB + i + 1)
                wait(act, pt_done, XB * (a * NB + i))
                act.activation(p_buf[:, 0:N], s_buf[:, 0:N], ACT.Exp, bias=nb[:, 0:1],
                               scale=1.0 if a else 2.0, accum_out=rowsum[:, u:u + 1]).then_inc(exp_done, 1)

            def p_hi_part(i, a):
                for b in range(XB):
                    n = min(PER_BANK, NB - PER_BANK * b) * P
                    wait(act, pt_done, XB * (a * NB + i) + b + 1)
                    if b == 0:
                        wait(act, hi_used, a * NB + i)
                        wait(act, plo_done, XB * (a * NB + i))
                    act.activation(pt_hi[:, b * BANK:b * BANK + n], ps_x[:, b, 0:n], ACT.Copy).then_inc(phi_done, 1)

            def attention(a, before_last=None):
                t_hi_part(0, 2 * P, a)
                exp(0, 0, a)
                with act.Fori(0, (NB - 3) // 2, 1) as k:
                    i = 2 * k
                    p_hi_part(i, a)
                    exp(i + 1, 1, a)
                    t_hi_part(k + 1, 2 * P, a)
                    p_hi_part(i + 1, a)
                    exp(i + 2, 0, a)
                p_hi_part(NB - 3, a)
                exp(NB - 2, 1, a)
                t_hi_part(PAIRS - 1, P, a)
                p_hi_part(NB - 2, a)
                exp(NB - 1, 0, a)
                if before_last:
                    before_last()
                p_hi_part(NB - 1, a)

            act.wait_ge(prep_cp, 4)
            split_w(wa_hi[:, :, 0:D], gram[:, :, :], 0)
            split_w(wb_hi[:, :, :], wv_sb[:, :, :], 0)
            project_all(0)

            def weights1():
                act.wait_ge(prep_v, 6)
                wait(act, proj_done, NB)
                act.wait_ge(t_done, PAIRS)
                split_w(wa_hi[:, :, :], wsa_sb[:, :, :], 0)
                split_w(wb_hi[:, :, :], wg_sb[:, :, :], 0)
                split_w(wl_hi[:, :, :], wl_sb[:, :, :], 0)

            attention(0, weights1)

            project_all(1)

            def adj_hi(i):
                wait(act, ahi_used, i)
                wait(act, alo_done, i)
                act.activation(at_hi[:, :], adjT_sb[:, i, :], ACT.Copy).then_inc(ahi_done, 1)

            def exp1(i):
                wait(act, leaky_done, i + 1)
                wait(act, plo1_done, i)
                act.activation(p_buf[:, :], s_buf[:, :], ACT.Exp, scale=-1.0 / TINY).then_inc(exp1_done, 1)

            def p1_hi(i):
                wait(act, exp1_done, i + 1)
                wait(act, hi1_used, i)
                act.activation(pt_hi[:, :], p_buf[:, :], ACT.Copy).then_inc(phi1_done, 1)

            def gate_exp(i):
                wait(act, zz_done, 2 * i + 2)
                act.activation(ez[:, :], zzb[:, :], ACT.Exp, scale=-1.0).then_inc(ez_done, 1)

            def tanh(i):
                wait(act, z1_done, i + 1)
                wait(act, x1_added, i)
                act.activation(th_buf[:, :], t2_buf[:, :], ACT.Tanh, scale=0.5).then_inc(th_done, 1)

            def t1(i):
                wait(act, rden_done, i + 1)
                act.activation(t1_buf[:, :], ps_o[:, 0:D], ACT.Copy, scale=rden[:, 0:1]).then_inc(t1_done, 1)

            act.wait_ge(adjT_in, 16)
            exp1(0)
            p1_hi(0)
            adj_hi(0)
            exp1(1)
            p1_hi(1)
            t1(0)

            def step1(i, first, second):
                if first:
                    adj_hi(i + 1)
                gate_exp(i)
                if second:
                    exp1(i + 2)
                tanh(i)
                if second:
                    p1_hi(i + 2)
                if first:
                    t1(i + 1)

            with act.Fori(0, NB - 2, 1) as i:
                step1(i, True, True)
            step1(NB - 2, True, False)
            act.wait_ge(w2_in, 16)
            wait(act, proj_done, 2 * NB)
            split_w(wa_hi[:, :, 0:D], w2_sb[:, :, :], 0)
            step1(NB - 1, False, False)

            project_all(2)
            wait(act, proj_done, 3 * NB)
            act.wait_ge(prep_cp, 6)
            act.wait_ge(w3_in, 16)
            split_w(wa_hi[:, :, 0:D], gram[:, :, :], 0)
            split_w(wb_hi[:, :, 0:D], w3_sb[:, :, :], 0)
            project_all(3)
            attention(1)

        @block.vector
        def _(dve):
            def split_w(dst, src, hi, n):
                dve.wait_ge(w_hi_set, n)
                dve.tensor_tensor(dst, src, f(hi), ALU.subtract).then_inc(w_lo_set, 1)

            def ln_stats(i, base):
                wait_apart(dve, mv_done, base + i)
                dve.bn_stats(stats[:, :], x_sb[:, i, :]).then_inc(stats_done, 1)
                wait(dve, ln_done, base + i)
                wait_apart(dve, stats_done, base + i + 1)
                dve.bn_aggr(mv[:, :], stats[:, :]).then_inc(mv_done, 1)

            def z(i, layer):
                wait(dve, ln_done, layer * NB + i + 1)
                if i >= 2:
                    wait(dve, zt_done, layer * NB + i - 1)
                dve.tensor_scalar(z_buf[:, i % 2, :], x_sb[:, i, :], mean_all[:, i:i + 1], rstd_all[:, i:i + 1],
                                  ALU.subtract, ALU.mult).then_inc(z_done, 1)

            def h_lo_part(i, layer):
                wait(dve, hhi_done, layer * NB + i + 1)
                hi, lo = h_block(i, layer)
                dve.scalar_tensor_tensor(out=lo, in0=ps_x[:, i % 2, 0:D].rearrange("p (c n) -> p c n", c=C),
                                         scalar=0.0, in1=f(hi), op0=ALU.max, op1=ALU.subtract).then_inc(hlo_done, 1)

            def bias(i, layer):
                u = i % 2
                wait(dve, proj_done, layer * NB + i + 1)
                wait(dve, vlo_done, {0: 0, 2: 3 * NB}[layer] + i - 1)
                if layer == 0:
                    dve.tensor_scalar(r_all[:, bass.ds(i, 1)], ps_s[:, u, D:D + 1], bqc[:, 0:1], None, ALU.add)
                dve.tensor_tensor(vb_buf[:, u, :], ps_s[:, u, 0:D], bv_row if layer == 0 else b2_row,
                                  ALU.add).then_inc(biased, 1)

            def v_lo_part(i, layer):
                u = i % 2
                if layer == 1:
                    wait(dve, vhi_done, NB + 2 * i + 1)
                    dve.tensor_tensor(g[1][:, i, :], ps_pair[u][:, 0:W], f(g[0][:, i, :]), ALU.subtract).then_inc(
                        vlo_done, 1)
                    wait(dve, vhi_done, NB + 2 * i + 2)
                    dve.tensor_scalar(right_all[:, bass.ds(i, 1)], ps_s[:, u, D:D + 1], TINY, None, ALU.mult)
                    dve.tensor_tensor(ext_all[:, i, :], ps_s[:, u, D + 1:D + 3], bab, ALU.add)
                    dve.tensor_tensor(v_lo[:, i, 0:D], ps_s[:, u, 0:D], f(v_hi[:, i, 0:D]),
                                      ALU.subtract).then_inc(vlo_done, 1)
                elif layer == 3:
                    wait(dve, vhi_done, 4 * NB + i + 1)
                    dve.tensor_tensor(v_lo[:, i, 0:D], ps_s[:, u, 0:D], f(v_hi[:, i, 0:D]),
                                      ALU.subtract).then_inc(vlo_done, 1)
                else:
                    wait(dve, vhi_done, (3 * NB if layer else 0) + i + 1)
                    dve.tensor_tensor(v_lo[:, i, 0:D], vb_buf[:, u, :], f(v_hi[:, i, 0:D]),
                                      ALU.subtract).then_inc(vlo_done, 1)

            def project_ahead(layer):
                z(0, layer)
                z(1, layer)

            def project_all(layer):
                z(2, layer)
                h_lo_part(0, layer)
                h_lo_part(1, layer)
                for i in range(NB + 1):
                    if i >= 1 and layer in (0, 2):
                        bias(i - 1, layer)
                    if i + 3 < NB:
                        z(i + 3, layer)
                    if i >= 1:
                        v_lo_part(i - 1, layer)
                    if i + 2 < NB:
                        h_lo_part(i + 2, layer)

            def t_lo_part(pair, n, a):
                wait(dve, thi_done, a * PAIRS + pair + 1)
                for c in range(C):
                    src = ps_t[:, c * D:c * D + n]
                    if a == 0:
                        ins = dve.scalar_tensor_tensor(out=t_lo[:, c, 0:n], in0=src, scalar=bqk[:, c:c + 1],
                                                       in1=f(t_hi[:, c, 0:n]), op0=ALU.add, op1=ALU.subtract)
                    else:
                        ins = dve.tensor_tensor(t_lo[:, c, 0:n], src, f(t_hi[:, c, 0:n]), ALU.subtract)
                ins.then_inc(tlo_done, 1)

            def mask_rows(i, u, half_i, a):
                if a == 0:
                    wait(dve, adj_in[u], 16 * (half_i + 1))
                    wait(dve, counted, i + 1)
                    dve.tensor_scalar(m_tmp[:, 0:N], a_buf[u][:, 0:N], 0.0, None,
                                      ALU.not_equal).then_inc(nonzero_done, 1)
                else:
                    wait(dve, eye_added, i + 1)
                    dve.tensor_scalar(m_buf[u][:, 0:N], a_buf[u][:, 0:N], 0.0, -BIG, ALU.is_le,
                                      ALU.mult).then_inc(mask3_done, 1)

            def add_adj(i, u, half_i, a):
                if a == 0:
                    wait(dve, adj_in[u], 16 * (half_i + 1))
                else:
                    wait(dve, mask3_done, i + 1)
                wait(dve, exp_done, a * NB + i)
                extra = a_buf[u] if a == 0 else m_buf[u]
                for n, (at, size) in enumerate(SCORE_CHUNKS):
                    wait_apart(dve, scored, 3 * (a * NB + i) + n + 1)
                    dve.tensor_tensor_reduce(s_buf[:, at:at + size], ps_s[:, n, 0:size],
                                             extra[:, at:at + size] if a == 0 else f(extra[:, at:at + size]),
                                             1.0, -3.4e38, ALU.add, ALU.max, mx3[:, n:n + 1]).then_inc(added, 1)
                wait(dve, added, 3 * (a * NB + i) + 3)
                dve.tensor_reduce(mx[:, :], mx3[:, 0:3], AX_X, ALU.max).then_inc(maxed, 1)
                wait(dve, maxed, a * NB + i + 1)
                if a == 0:
                    r = r_all[:, bass.ds(i, 1)]
                    dve.tensor_scalar(mr[:, :], mx[:, :], r, None, ALU.add).then_inc(shifted, 1)
                    wait(dve, shifted, i + 1)
                    dve.tensor_scalar(nb[:, :], mr[:, :], r, -2.0, ALU.subtract, ALU.mult).then_inc(nb_done, 1)
                else:
                    dve.tensor_scalar(nb[:, :], mx[:, :], -1.0, None, ALU.mult).then_inc(nb_done, 1)

            def p_lo_part(i, a):
                for b in range(XB):
                    n = min(PER_BANK, NB - PER_BANK * b) * P
                    wait(dve, phi_done, XB * (a * NB + i) + b + 1)
                    dve.tensor_tensor(pt_lo[:, b * BANK:b * BANK + n], ps_x[:, b, 0:n],
                                      f(pt_hi[:, b * BANK:b * BANK + n]), ALU.subtract).then_inc(plo_done, 1)

            def add_out(i, u, a):
                wait(dve, x_added, a * NB + i)
                wait(dve, exp_done, a * NB + i + 1)
                dve.reciprocal(rinv[:, :], rowsum[:, u:u + 1]).then_inc(rinv_done, 1)
                wait(dve, rinv_done, a * NB + i + 1)
                wait(dve, agg_done, a * NB + i + 1)
                dve.scalar_tensor_tensor(out=x_sb[:, i, :], in0=ps_o[:, 0:D], scalar=rinv[:, 0:1], in1=x_sb[:, i, :],
                                         op0=ALU.mult, op1=ALU.add).then_inc(x_added, 1)
                if a == 0:
                    wait_apart(dve, x_added, i + 1)
                    ln_stats(i, NB)

            def attention(a, before_last=None):
                t_lo_part(0, 2 * P, a)
                mask_rows(0, 0, 0, a)
                add_adj(0, 0, 0, a)
                with dve.Fori(0, (NB - 3) // 2, 1) as k:
                    i = 2 * k
                    mask_rows(i + 1, 1, k, a)
                    p_lo_part(i, a)
                    add_adj(i + 1, 1, k, a)
                    t_lo_part(k + 1, 2 * P, a)
                    add_out(i, 0, a)
                    mask_rows(i + 2, 0, k + 1, a)
                    p_lo_part(i + 1, a)
                    add_adj(i + 2, 0, k + 1, a)
                    add_out(i + 1, 1, a)
                mask_rows(NB - 2, 1, (NB - 2) // 2, a)
                p_lo_part(NB - 3, a)
                add_adj(NB - 2, 1, (NB - 2) // 2, a)
                t_lo_part(PAIRS - 1, P, a)
                add_out(NB - 3, 0, a)
                mask_rows(NB - 1, 0, (NB - 1) // 2, a)
                p_lo_part(NB - 2, a)
                add_adj(NB - 1, 0, (NB - 1) // 2, a)
                add_out(NB - 2, 1, a)
                p_lo_part(NB - 1, a)
                if before_last:
                    before_last()
                add_out(NB - 1, 0, a)

            dve.memset(f(v_hi[:, :, D:D + 1]), 1.0)
            dve.memset(f(v_hi[:, :, D + 1:W]), 0.0)
            dve.memset(f(v_lo[:, :, D:W]), 0.0)
            dve.memset(wv_sb[:, :, D + 1:W], 0.0)
            dve.memset(deg[:, :], 1.0)
            dve.memset(ones[:, :], 1.0)
            dve.wait_ge(v_in, 48)
            for c in range(C):
                dve.tensor_copy(bq_rep[:, c, :], bq_col[:, c:c + 1].broadcast_to((P, P)))
            dve.tensor_copy(wg_sb[:, :, D:D + 1], cols_sb[:, 2, :].unsqueeze(2))
            dve.tensor_copy(wg_sb[:, :, D + 1:W], cols_sb[:, 4, :].unsqueeze(2))
            dve.tensor_copy(wsa_sb[:, :, D + 1:D + 2], cols_sb[:, 3, :].unsqueeze(2))
            dve.tensor_copy(wsa_sb[:, :, D + 2:D + 3], cols_sb[:, 5, :].unsqueeze(2))
            dve.memset(wsa_sb[:, :, D + 3:WA], 0.0).then_inc(prep_v, 1)
            start_counts(dve, plo_done, mv_done, vlo_done, x_added, hlo_done, t2_done, zz_done)
            for part, (b0, b1) in enumerate(X_PARTS):
                final = part == len(X_PARTS) - 1
                dve.wait_ge(x_in[part], 32 if final else 16)
                for i in range(b0, NB if final else b1):
                    wait(dve, mv_done, i)
                    dve.bn_stats(stats[:, :], x_sb[:, i, :]).then_inc(stats_done, 1)
                    dve.wait_ge(stats_done, i + 1)
                    dve.bn_aggr(mv_all[:, i, :], stats[:, :]).then_inc(mv_done, 1)
            dve.wait_ge(prep_mm, 1)
            dve.tensor_scalar(gram[:, :, :], ps_s[:, 0, :].rearrange("p (c n) -> p c n", c=C), HALF_SCALE, None,
                              ALU.mult).then_inc(prep_cp, 1)
            dve.wait_ge(prep_mm, 2)
            dve.tensor_scalar(wv_sb[:, :, D:D + 1], ps_s[:, 1, 0:C].unsqueeze(2), HALF_SCALE, None,
                              ALU.mult).then_inc(prep_cp, 1)
            dve.tensor_scalar(bqk[:, :], ps_s[:, 1, C:2 * C], HALF_SCALE, None, ALU.mult).then_inc(prep_cp, 1)
            dve.tensor_scalar(bqc[:, :], ps_s[:, 1, 2 * C:2 * C + 1], HALF_SCALE, None, ALU.mult).then_inc(prep_cp, 1)
            dve.wait_ge(prep_mm, 3)
            dve.tensor_copy(u3T_sb[:, :, :], ps_s[:, 2, :].rearrange("p (c n) -> p c n", c=C)).then_inc(prep_cp, 1)
            split_w(wa_lo[:, :, 0:D], gram[:, :, :], wa_hi[:, :, 0:D], 1)
            split_w(wb_lo[:, :, :], wv_sb[:, :, :], wb_hi[:, :, :], 2)
            dve.wait_ge(prep_mm, 4)
            dve.wait_ge(w_lo_set, 1)
            dve.tensor_copy(gram[:, :, :], ps_x[:, 2, :].rearrange("p (c n) -> p c n", c=C)).then_inc(prep_cp, 1)
            dve.wait_ge(lw_in, 64)
            for c in range(C):
                for s in range(2):
                    dve.wait_ge(prep_v, 1 + 2 * c + s)
                    dve.tensor_tensor_reduce(vb_buf[:, s, :], wsa_sb[:, c, 0:D],
                                             asa_sb[:, s, :], 1.0, 0.0, ALU.mult, ALU.add,
                                             wlr[:, c, s:s + 1]).then_inc(prep_v, 1)
            project_ahead(0)
            project_all(0)
            dve.wait_ge(prep_v, 5)
            dve.tensor_copy(wl_sb[:, :, :], wlr[:, :, 0:1].broadcast_to((P, C, P)))
            dve.tensor_copy(wsa_sb[:, :, D:D + 1], wlr[:, :, 1:2]).then_inc(prep_v, 1)

            def ahead1():
                dve.wait_ge(prep_v, 6)
                split_w(wa_lo[:, :, :], wsa_sb[:, :, :], wa_hi[:, :, :], 3)
                split_w(wb_lo[:, :, :], wg_sb[:, :, :], wb_hi[:, :, :], 4)
                split_w(wl_lo[:, :, :], wl_sb[:, :, :], wl_hi[:, :, :], 5)
                project_ahead(1)

            attention(0, ahead1)

            project_all(1)

            def masked(i):
                wait(dve, sums_done, i + 1)
                wait(dve, exp1_done, i)
                dve.scalar_tensor_tensor(out=s_buf[:, :], in0=adjT_sb[:, i, :], scalar=0.0, in1=sums_buf[:, :],
                                         op0=ALU.is_equal, op1=ALU.add).then_inc(masked_done, 1)

            def leaky(i):
                wait(dve, masked_done, i + 1)
                dve.scalar_tensor_tensor(out=s_buf[:, :], in0=s_buf[:, :], scalar=0.01, in1=s_buf[:, :],
                                         op0=ALU.mult, op1=ALU.max).then_inc(leaky_done, 1)

            def p1_lo(i):
                wait(dve, phi1_done, i + 1)
                dve.tensor_tensor(pt_lo[:, :], p_buf[:, :], f(pt_hi[:, :]), ALU.subtract).then_inc(plo1_done, 1)

            def inv_den(i):
                wait(dve, xa_done, i + 1)
                wait(dve, t1_done, i)
                dve.tensor_scalar(den[:, :], ps_o[:, D:D + 1], EPS, None, ALU.add).then_inc(den_set, 1)
                wait(dve, den_set, i + 1)
                dve.reciprocal(rden[:, :], den[:, :]).then_inc(rden_done, 1)

            def gates_in(i):
                wait(dve, xb_done, i + 1)
                wait(dve, th_done, i)
                dve.tensor_tensor(zz[:, :], ps_t[:, D:W], ext_all[:, i, :], ALU.add).then_inc(zz_done, 1)
                dve.tensor_tensor(t2_buf[:, :], ps_t[:, 0:D], bg_row, ALU.add).then_inc(t2_done, 1)
                wait(dve, zz_done, 2 * i + 1)
                dve.tensor_scalar(zzb[:, :], zz[:, :], -87.0, None, ALU.max).then_inc(zz_done, 1)

            def gate(i):
                wait(dve, ez_done, i + 1)
                dve.tensor_scalar(al[:, :], ez[:, :], 1.0, None, ALU.add).then_inc(al_step, 1)
                wait(dve, al_step, 3 * i + 1)
                dve.reciprocal(al[:, :], al[:, :]).then_inc(al_step, 1)
                wait(dve, al_step, 3 * i + 2)
                wait(dve, t2_done, i + 1)
                wait(dve, t1_done, i + 1)
                dve.tensor_scalar(t1_buf[:, :], t1_buf[:, :], al[:, 0:1], None, ALU.mult).then_inc(al_step, 1)
                wait(dve, al_step, 3 * i + 3)
                dve.scalar_tensor_tensor(out=t2_buf[:, :], in0=t2_buf[:, :], scalar=al[:, 1:2], in1=t1_buf[:, :],
                                         op0=ALU.mult, op1=ALU.add).then_inc(z1_done, 1)

            def stats1(i):
                wait_apart(dve, x1_added, i + 1)
                ln_stats(i, 2 * NB)

            dve.wait_ge(adjT_in, 16)
            masked(0)
            leaky(0)
            p1_lo(0)
            masked(1)
            leaky(1)
            inv_den(0)
            p1_lo(1)

            def step1(i, first, second):
                gates_in(i)
                if second:
                    masked(i + 2)
                if second:
                    leaky(i + 2)
                gate(i)
                if first:
                    inv_den(i + 1)
                if second:
                    p1_lo(i + 2)
                stats1(i)

            with dve.Fori(0, NB - 2, 1) as i:
                step1(i, True, True)
            step1(NB - 2, True, False)
            split_w(wa_lo[:, :, 0:D], w2_sb[:, :, :], wa_hi[:, :, 0:D], 6)
            project_ahead(2)
            step1(NB - 1, False, False)
            dve.wait_ge(deg_mm, 1)
            dve.tensor_copy(deg[:, 0:NB - 1], ps_x[:, 2, 0:NB - 1])
            dve.tensor_copy(deg[0:LAST, NB - 1:NB], ps_x[0:LAST, 2, NB - 1:NB]).then_inc(deg_done, 1)
            dve.wait_ge(deg_done, 1)
            dve.reciprocal(rdeg[:, :], deg[:, :]).then_inc(deg_done, 1)

            project_all(2)

            def mask2(i, u):
                if not isinstance(i, int) or i >= 2:
                    wait(dve, agg2_done, i - 1)
                dve.tensor_scalar(m_buf[u][:, :], adjT_sb[:, i, :], 0.0, None, ALU.not_equal).then_inc(mask2_done, 1)

            def out2(i, u):
                wait(dve, agg2_done, i + 1)
                dve.scalar_tensor_tensor(out=x_sb[:, i, :], in0=ps_pair[u][:, 0:D], scalar=rdeg[:, bass.ds(i, 1)],
                                         in1=x_sb[:, i, :], op0=ALU.mult, op1=ALU.add).then_inc(x2_added, 1)
                wait_apart(dve, x2_added, i + 1)
                ln_stats(i, 3 * NB)

            dve.wait_ge(deg_done, 2)
            mask2(0, 0)
            with dve.Fori(0, (NB - 1) // 2, 1) as k:
                for u in range(2):
                    mask2(2 * k + u + 1, 1 - u)
                    out2(2 * k + u, u)
            split_w(wa_lo[:, :, 0:D], gram[:, :, :], wa_hi[:, :, 0:D], 7)
            split_w(wb_lo[:, :, 0:D], w3_sb[:, :, :], wb_hi[:, :, 0:D], 8)
            project_ahead(3)
            out2(NB - 1, 0)

            project_all(3)
            attention(1)

        @block.tensor
        def _(pe):
            start_counts(pe, agg_done, proj_done, agg2_done, hi_used, hi1_used, ahi_used)
            pe.wait_ge(w_in, 48)
            for m in range(C):
                for c in range(C):
                    ins = pe.matmul(ps_s[:, 0, m * D:(m + 1) * D], wq_sb[:, c, m * P:(m + 1) * P], wk_sb[:, c, :],
                                    start=(c == 0), stop=(c == C - 1))
            ins.then_inc(prep_mm, 1)
            pe.wait_ge(prep_v, 1)
            for m in range(C):
                for col, (w, b) in ((m, (wq_sb, bk_col)), (C + m, (wk_sb, bq_col))):
                    for c in range(C):
                        pe.matmul(ps_s[:, 1, col:col + 1], w[:, c, m * P:(m + 1) * P], b[:, c:c + 1],
                                  start=(c == 0), stop=(c == C - 1))
            for c in range(C):
                ins = pe.matmul(ps_s[:, 1, 2 * C:2 * C + 1], bq_rep[:, c, :], bk_col[:, c:c + 1],
                                start=(c == 0), stop=(c == C - 1))
            ins.then_inc(prep_mm, 1)
            pe.wait_ge(lw_in, 64)
            for m in range(C):
                for c in range(C):
                    ins = pe.matmul(ps_s[:, 2, m * D:(m + 1) * D], u3T_sb[:, c, m * P:(m + 1) * P], w3T_sb[:, c, :],
                                    start=(c == 0), stop=(c == C - 1))
            ins.then_inc(prep_mm, 1)
            pe.wait_ge(prep_cp, 5)
            for m in range(C):
                for c in range(C):
                    ins = pe.matmul(ps_x[:, 2, m * D:(m + 1) * D], w3T_sb[:, c, m * P:(m + 1) * P], u3T_sb[:, c, :],
                                    start=(c == 0), stop=(c == C - 1))
            ins.then_inc(prep_mm, 1)
            pe.wait_ge(ident_in, 16)

            def transpose_z(i, layer):
                wait(pe, z_done, layer * NB + i + 1)
                if i >= 2:
                    wait(pe, hlo_done, layer * NB + i - 1)
                u = i % 2
                for c in range(C):
                    ins = pe.transpose(ps_x[:, u, c * P:(c + 1) * P], z_buf[:, u, c * P:(c + 1) * P], ident[:, :])
                ins.then_inc(zt_done, 1)

            def project(i, layer):
                u = i % 2
                wait(pe, hlo_done, layer * NB + i + 1)
                if i >= 2:
                    base = {0: 0, 1: NB, 2: 3 * NB, 3: 4 * NB}[layer]
                    wait(pe, vlo_done, base + (2 if layer == 1 else 1) * (i - 1))
                hi, lo = h_block(i, layer)
                for c in range(C):
                    h = hi[:, c, :], lo[:, c, :]
                    wa = wa_hi[:, c, :], wa_lo[:, c, :]
                    wb = wb_hi[:, c, :], wb_lo[:, c, :]
                    a, b = (c == 0), (c == C - 1)
                    if layer == 0:
                        ins = products(pe, ps_s[:, u, 0:W], h, wb, a, b)
                    elif layer == 1:
                        products(pe, ps_s[:, u, 0:WA], h, wa, a, b)
                        products(pe, ps_pair[u][:, 0:W], h, wb, a, b)
                        ins = products(pe, ps_left[u][:, 0:P], (wl_hi[:, c, :], wl_lo[:, c, :]), h, a, b)
                    elif layer == 2:
                        ins = products(pe, ps_s[:, u, 0:D], h, [w[:, 0:D] for w in wa], a, b)
                    else:
                        ins = products(pe, ps_s[:, u, 0:D], h, [w[:, 0:D] for w in wb], a, b)
                ins.then_inc(proj_done, 1)

            def project_all(layer, weights):
                transpose_z(0, layer)
                transpose_z(1, layer)
                pe.wait_ge(w_lo_set, weights)
                for i in range(NB):
                    if i + 2 < NB:
                        transpose_z(i + 2, layer)
                    project(i, layer)

            def make_t(pair, at, n, a):
                wait(pe, tlo_done, a * PAIRS + pair)
                for m in range(C):
                    for c in range(C):
                        ins = products(pe, ps_t[:, m * D:m * D + n],
                                       (wa_hi[:, c, m * P:(m + 1) * P], wa_lo[:, c, m * P:(m + 1) * P]),
                                       (hT[0][:, c, bass.ds(at, n)], hT[1][:, c, bass.ds(at, n)]), c == 0, c == C - 1)
                ins.then_inc(t_done, 1)

            def score(i, u, pair, a):
                wait(pe, tlo_done, a * PAIRS + pair + 1)
                mine = slice(u * P, (u + 1) * P)
                for n, (at, size) in enumerate(SCORE_CHUNKS):
                    wait(pe, added, 3 * (a * NB + i - 1) + n + 1)
                    for c in range(C):
                        ins = products(pe, ps_s[:, n, 0:size], (t_hi[:, c, mine], t_lo[:, c, mine]),
                                       (hT[0][:, c, at:at + size], hT[1][:, c, at:at + size]), c == 0, c == C - 1)
                    ins.then_inc(scored, 1)

            def transpose_p(i, a):
                if a == 0:
                    wait(pe, exp_done, i + 1)
                else:
                    wait(pe, p_done, i + 1)
                for b in range(XB):
                    wait(pe, plo_done, XB * (a * NB + i - 1) + b + 1)
                    n = min(PER_BANK, NB - PER_BANK * b)
                    for t in range(n):
                        j = PER_BANK * b + t
                        ins = pe.transpose(ps_x[:, b, t * P:(t + 1) * P], p_buf[:, j * P:(j + 1) * P], ident[:, :])
                    ins.then_inc(pt_done, 1)

            def weighted(out_ap, p, v, wait_lo, hi_sem):
                for j in range(NB):
                    at = slice(j * P, (j + 1) * P)
                    pe.matmul(out_ap, p[0][:, at], v[0](j), start=(j == 0), stop=False)
                    ins = pe.matmul(out_ap, p[0][:, at], v[1](j), start=False, stop=False)
                ins.then_inc(hi_sem, 1)
                wait_lo()
                for j in range(NB):
                    ins = pe.matmul(out_ap, p[1][:, j * P:(j + 1) * P], v[0](j), start=False, stop=(j == NB - 1))
                return ins

            def aggregate(i, a):
                wait(pe, x_added, a * NB + i)
                wait(pe, phi_done, XB * (a * NB + i) + XB)
                weighted(ps_o[:, 0:D], (pt_hi, pt_lo), (lambda j: v_hi[:, j, 0:D], lambda j: v_lo[:, j, 0:D]),
                         lambda: wait(pe, plo_done, XB * (a * NB + i) + XB), hi_used).then_inc(agg_done, 1)

            def attention(a):
                make_t(0, 0, 2 * P, a)
                score(0, 0, 0, a)
                transpose_p(0, a)
                wait(pe, vlo_done, 5 * NB if a else NB)
                with pe.Fori(0, (NB - 3) // 2, 1) as k:
                    i = 2 * k
                    score(i + 1, 1, k, a)
                    make_t(k + 1, 2 * P * (k + 1), 2 * P, a)
                    aggregate(i, a)
                    transpose_p(i + 1, a)
                    score(i + 2, 0, k + 1, a)
                    aggregate(i + 1, a)
                    transpose_p(i + 2, a)
                score(NB - 2, 1, PAIRS - 2, a)
                make_t(PAIRS - 1, (NB - 1) * P, P, a)
                aggregate(NB - 3, a)
                transpose_p(NB - 2, a)
                score(NB - 1, 0, PAIRS - 1, a)
                aggregate(NB - 2, a)
                transpose_p(NB - 1, a)
                aggregate(NB - 1, a)

            project_all(0, 2)
            attention(0)
            project_all(1, 5)

            def aggregate1(i):
                wait(pe, phi1_done, i + 1)
                wait(pe, t1_done, i)
                weighted(ps_o[:, 0:W], (pt_hi, pt_lo), (lambda j: v_hi[:, j, :], lambda j: v_lo[:, j, :]),
                         lambda: wait(pe, plo1_done, i + 1), hi1_used).then_inc(xa_done, 1)
                wait(pe, ahi_done, i + 1)
                wait(pe, t2_done, i)
                wait(pe, zz_done, 2 * i)
                weighted(ps_t[:, 0:W], (at_hi, at_lo), (lambda j: g[0][:, j, :], lambda j: g[1][:, j, :]),
                         lambda: wait(pe, alo_done, i + 1), ahi_used).then_inc(xb_done, 1)

            wait(pe, vlo_done, 3 * NB)
            with pe.Fori(0, NB, 1) as i:
                aggregate1(i)
            pe.wait_ge(counted, NB + 1)
            for j in range(NB):
                w = min(P, N - j * P)
                ins = pe.matmul(ps_x[0:w, 2, j:j + 1], f(cnt[:, j * P:j * P + w]), ones[:, :], start=True, stop=True)
            ins.then_inc(deg_mm, 1)

            project_all(2, 6)

            def aggregate2(i, u, k):
                wait(pe, mask2_done, i + 1)
                for j in range(NB):
                    for part in (v_hi, v_lo):
                        ins = pe.matmul(ps_pair[u][:, 0:D], m_buf[u][:, j * P:(j + 1) * P], part[:, j, 0:D],
                                        start=(j == 0 and part is v_hi), stop=(j == NB - 1 and part is v_lo))
                ins.then_inc(agg2_done, 1)

            wait(pe, vlo_done, 4 * NB)
            pairs(pe, NB, aggregate2)

            project_all(3, 8)
            attention(1)


_INS = ["x", "adj", "adjT", "wq", "wk", "wvT", "wsa", "wgcn", "w2", "w3", "w3T", "u3T", "asa", "cols", "rows", "eye"]


def kernel(**inputs):
    import numpy as _np
    import concourse.bacc as _bacc
    from concourse import mybir as _mybir
    from concourse.bass_utils import run_bass_kernel_spmd as _run

    a = {k: _np.asarray(v) for k, v in inputs.items()}
    padded = _np.zeros((NP, NP), a["adj"].dtype)
    padded[:N, :N] = a["adj"]
    adjT = padded.reshape(NB, P, NB, P).transpose(0, 3, 2, 1).reshape(NB, P, NB * P)
    laid = {
        "x": a["x"], "adj": a["adj"], "adjT": adjT,
        "wq": a["L0_gnn_Wq"], "wk": a["L0_gnn_Wk"], "wvT": a["L0_gnn_Wv"].T,
        "wsa": a["L1_gnn_W_sa"], "wgcn": a["L1_gnn_W_gcnb"], "w2": a["L2_gnn_W"],
        "w3": a["L3_gnn_W"], "w3T": a["L3_gnn_W"].T, "u3T": a["L3_gnn_U"].T,
        "asa": a["L1_gnn_a_sa"].reshape(2, D),
        "cols": _np.stack([a["L0_gnn_bq"], a["L0_gnn_bk"], a["L1_gnn_Wa"][0, :D], a["L1_gnn_Wa"][0, D:],
                           a["L1_gnn_Wb"][0, :D], a["L1_gnn_Wb"][0, D:]]).reshape(6, C, P).transpose(2, 0, 1),
        "rows": _np.concatenate([a["L0_gnn_bv"], a["L2_gnn_b"], a["L1_gnn_b_gcnb"], a["L1_gnn_ba"], a["L1_gnn_bb"]]),
        "eye": _np.eye(P, dtype=a["adj"].dtype),
    }
    nc = _bacc.Bacc("TRN2", target_bir_lowering=False, num_devices=1, dynamic_dma_scratch_size=8192)
    arrays, args = {}, []
    for name in _INS:
        v = _np.ascontiguousarray(laid[name])
        arrays[f"in_{name}_dram"] = v
        args.append(nc.dram_tensor(f"in_{name}_dram", v.shape, _mybir.dt.from_np(v.dtype), kind="ExternalInput").ap())
    args.append(nc.dram_tensor("out_dram", (N, D), _mybir.dt.float32, kind="ExternalOutput").ap())
    graph_layers_kernel(nc, *args)
    r = _run(nc, [arrays], core_ids=[0])
    return r.results[0]["out_dram"]
```

```python
from contextlib import ExitStack

import concourse.bass as bass
from concourse import mybir

ALU = mybir.AluOpType
ACT = mybir.ActivationFunctionType
F32 = mybir.dt.float32
F32R = mybir.dt.float32r
AX_X = mybir.AxisListType.X

P = 128
N = 1354
D = 256
C = D // P
NB = -(-N // P)
NP = NB * P
LAST = N - (NB - 1) * P
W = D + 2
WA = D + 4
BANK = 512
SCORE_CHUNKS = [(0, 452), (452, 452), (904, N - 904)]
PAIRS = (NB + 1) // 2
XB = 3
PER_BANK = 4
P_CHUNKS = [(b * BANK, min((b + 1) * BANK, N)) for b in range(XB)]
X_PARTS = [(0, 3), (3, 7), (7, NB - 1)]
EPS = 1e-5
BIG = 3.0e38
EARLY = NB - 3
T_STEP = NB - 2
TINY = 2.0 ** -60
HALF_SCALE = 0.5 * D ** -0.5


def graph_layers_kernel(nc, x, adj, adjT, wq, wk, wvT, wsa, wgcn, w2, w3, w3T, u3T, asa, cols, rows, eye, out):
    with ExitStack() as ctx:
        def sb(name, shape, dt=F32):
            return ctx.enter_context(nc.sbuf_tensor(name, shape, dt))

        def ps(name, shape):
            return ctx.enter_context(nc.psum_tensor(name, shape, F32))

        def sem(name):
            return ctx.enter_context(nc.semaphore(name))

        def f(ap):
            return ap.bitcast(F32)

        def tiles(ap):
            return ap.rearrange("p (t m) -> p t m", m=P)

        x_sb = sb("x_sb", [P, NB, D])
        adjT_sb = sb("adjT_sb", [P, NB, NB * P])
        hT_hi = sb("hT_hi", [P, NB * W], F32R)
        hT_lo = sb("hT_lo", [P, NB * W], F32R)
        v_hi = sb("v_hi", [P, NB, W], F32R)
        v_lo = sb("v_lo", [P, NB, W], F32R)
        wa_hi = sb("wa_hi", [P, C, WA], F32R)
        wa_lo = sb("wa_lo", [P, C, WA], F32R)
        wb_hi = sb("wb_hi", [P, C, W], F32R)
        wb_lo = sb("wb_lo", [P, C, W], F32R)
        wl_hi = sb("wl_hi", [P, C, P], F32R)
        wl_lo = sb("wl_lo", [P, C, P], F32R)
        wv_sb = sb("wv_sb", [P, C, W])
        wsa_sb = sb("wsa_sb", [P, C, WA])
        wg_sb = sb("wg_sb", [P, C, W])
        gram = sb("gram", [P, C, D])
        x_stats = sb("x_stats", [P, NB, 6])
        wl_sb = sb("wl_sb", [P, C, P])
        asa_sb = sb("asa_sb", [P, 2, D])
        rows_sb = sb("rows_sb", [P, 3 * D + 2])
        cols_sb = sb("cols_sb", [P, 6, C])
        wlr = sb("wlr", [P, C, 2])
        bqk = sb("bqk", [P, C])
        bqc = sb("bqc", [P, 1])
        bq_rep = sb("bq_rep", [P, C, P])
        ident = sb("ident", [P, P])
        a_buf = [sb(f"a_buf{u}", [P, NP]) for u in range(2)]
        m_buf = [sb(f"m_buf{u}", [P, NP], F32R) for u in range(2)]
        s_buf = sb("s_buf", [P, NP])
        p_buf = sb("p_buf", [P, NP])
        pt_hi = sb("pt_hi", [P, NP], F32R)
        pt_lo = sb("pt_lo", [P, NP], F32R)
        at_hi = sb("at_hi", [P, NP], F32R)
        at_lo = sb("at_lo", [P, NP], F32R)
        h_hi = sb("h_hi", [P, 3, C, P], F32R)
        h_lo = sb("h_lo", [P, 3, C, P], F32R)
        z_buf = sb("z_buf", [P, 2, D])
        t2_buf = sb("t2_buf", [P, 2, D])
        th_buf = sb("th_buf", [P, D])
        vb_buf = sb("vb_buf", [P, 2, D])
        stats = sb("stats", [P, 6])
        mv = sb("mv", [P, 2])
        veps = sb("veps", [P, 1])
        mhalf = sb("mhalf", [P, 1])
        negmean = sb("negmean", [P, 1])
        mr_all = sb("mr_all", [P, NB, 2])
        right_all = sb("right_all", [P, NB])
        ext_all = sb("ext_all", [P, NB, 2])
        ones = sb("ones", [P, 1])
        halves = sb("halves", [P, 1])
        r_all = sb("r_all", [P, NB])
        mx3 = sb("mx3", [P, 4])
        mx = sb("mx", [P, 1])
        mr = sb("mr", [P, 1])
        nb = sb("nb", [P, 1])
        rowsum3 = sb("rowsum3", [P, 2, XB])
        rowsum = sb("rowsum", [P, 1])
        rinv = sb("rinv", [P, 1])
        zz = sb("zz", [P, 2])
        zzb = sb("zzb", [P, 2])
        ez = sb("ez", [P, 2])
        al = sb("al", [P, 3])
        ral = sb("ral", [P, 3])
        sal = sb("sal", [P, 1])
        deg = sb("deg", [P, NB])
        rdeg = sb("rdeg", [P, NB])

        hT = [t[:, 0:C * NP].rearrange("p (c n) -> p c n", c=C) for t in (hT_hi, hT_lo)]
        g = [t[:, :].rearrange("p (b w) -> p b w", w=W) for t in (hT_hi, hT_lo)]
        slb = a_buf[0]
        s_pair = [s_buf, a_buf[1]]

        def h_block(i, layer):
            if layer in (0, 3):
                return [t[:, :, i * P:(i + 1) * P] for t in hT]
            return [t[:, i % 3, :, :] for t in (h_hi, h_lo)]

        def v_bank(i, layer):
            return ps_s[:, i % 2 if layer == 1 else i % 3, :]

        m_tmp, cnt = m_buf
        w2_sb, w3_sb = wv_sb[:, :, 0:D], wg_sb[:, :, 0:D]
        t_hi, t_lo = [h[:, 0:2, :, :].rearrange("p a c n -> p (a c n)").rearrange("p (c n) -> p c n", c=C)
                      for h in (h_hi, h_lo)]
        t1_buf = vb_buf[:, 0, :]
        wq_sb, wk_sb, w3T_sb, u3T_sb, gq, uw = [
            adjT_sb[:, n // 2, (n % 2) * C * D:(n % 2 + 1) * C * D].rearrange("p (c n) -> p c n", c=C)
            for n in range(6)]
        bv_row, b2_row, bg_row, bab = rows_sb[:, 0:D], rows_sb[:, D:2 * D], rows_sb[:, 2 * D:3 * D], rows_sb[:, 3 * D:]
        bq_col, bk_col = cols_sb[:, 0, :], cols_sb[:, 1, :]

        ps_s = ps("ps_s", [P, 3, BANK])
        ps_x = ps("ps_x", [P, XB, BANK])
        ps_o = ps("ps_o", [P, BANK])
        ps_t = ps("ps_t", [P, BANK])
        ps_pair = [ps_o, ps_t]
        ps_xa = [ps_o[:, :], ps_s[:, 0, :]]
        ps_xb = [ps_t[:, :], ps_s[:, 1, :]]
        ps_left = [ps_s[:, 2, :], ps_x[:, 2, :]]

        x_in = [sem(f"x_in{part}") for part in range(len(X_PARTS))]
        w_in, v_in, lw_in, adjT_in = (sem(n) for n in ("w_in", "v_in", "lw_in", "adjT_in"))
        w2_in, w3_in = sem("w2_in"), sem("w3_in")
        adj_in = [sem("adj_in0"), sem("adj_in1")]
        out_sent = sem("out_sent")
        passed = sem("passed")
        consts_set, pads_set, ident_in = sem("consts_set"), sem("pads_set"), sem("ident_in")
        prep_mm, prep_cp, prep_v = sem("prep_mm"), sem("prep_cp"), sem("prep_v")
        cols_in, wv_in, uw_set, gram_set = sem("cols_in"), sem("wv_in"), sem("uw_set"), sem("gram_set")
        w_hi_set, w_lo_set = sem("w_hi_set"), sem("w_lo_set")
        stats_done, mv_done, veps_set, ln_done = sem("stats_done"), sem("mv_done"), sem("veps_set"), sem("ln_done")
        z_done, zt_done, hhi_done, hlo_done = sem("z_done"), sem("zt_done"), sem("hhi_done"), sem("hlo_done")
        proj_done, biased = sem("proj_done"), sem("biased")
        vhi_done, vlo_done = sem("vhi_done"), sem("vlo_done")
        t_done, thi_done, tlo_done = sem("t_done"), sem("thi_done"), sem("tlo_done")
        scored, added, maxed, shifted, nb_done = (sem("scored"), sem("added"), sem("maxed"), sem("shifted"),
                                                  sem("nb_done"))
        exp_done, p_done, p_end_done, pt_done = sem("exp_done"), sem("p_done"), sem("p_end_done"), sem("pt_done")
        phi_done, plo_done, agg_done = sem("phi_done"), sem("plo_done"), sem("agg_done")
        hi_used, hi1_used, ahi_used = sem("hi_used"), sem("hi1_used"), sem("ahi_used")
        rinv_done, x_added = sem("rinv_done"), sem("x_added")
        rstd_set = sem("rstd_set")
        bv_added, summed = sem("bv_added"), sem("summed")
        eye_added, mask3_done = sem("eye_added"), sem("mask3_done")
        sums_done, masked_done, leaky_done, exp1_done = (sem("sums_done"), sem("masked_done"), sem("leaky_done"),
                                                         sem("exp1_done"))
        nonzero_done, deg_mm = sem("nonzero_done"), sem("deg_mm")
        phi1_done, plo1_done, ahi_done, alo_done = sem("phi1_done"), sem("plo1_done"), sem("ahi_done"), sem("alo_done")
        xa_done, xb_done, t1_done = sem("xa_done"), sem("xb_done"), sem("t1_done")
        zz_done, t2_done, ez_done = sem("zz_done"), sem("t2_done"), sem("ez_done")
        al_set, ral_done, sal_done, z1_done, th_done, half_done, counted = (
            sem(n) for n in ("al_set", "ral_done", "sal_done", "z1_done", "th_done", "half_done", "counted"))
        x1_added, deg_done, mask2_done, agg2_done, x2_added = (sem("x1_added"), sem("deg_done"), sem("mask2_done"),
                                                               sem("agg2_done"), sem("x2_added"))

        from_one = [agg_done, proj_done, x1_added, agg2_done, ln_done, mv_done, th_done, vlo_done, x_added, hlo_done,
                    t1_done, t2_done, zz_done, hi_used, hi1_used, ahi_used,
                    plo_done, rinv_done]

        def start_counts(eng, *sems):
            for s in sems:
                eng.sem_inc(s, 1)

        def wait(eng, s, value):
            if not (isinstance(value, int) and value <= 0):
                eng.wait_ge(s, value + 1 if any(s is t for t in from_one) else value)

        def wait_apart(eng, s, value):
            wait(eng, s, value)
            if not isinstance(value, int):
                eng.sem_inc(passed, 1)

        def products(eng, out_ap, lhs, rhs, first, last, skip=False):
            eng.matmul(out_ap, lhs[0], rhs[0], start=first, stop=False, skip_group_check=skip)
            eng.matmul(out_ap, lhs[0], rhs[1], start=False, stop=False, skip_group_check=skip)
            return eng.matmul(out_ap, lhs[1], rhs[0], start=False, stop=last, skip_group_check=skip)

        block = ctx.enter_context(nc.Block())

        @block.sync
        def _(sp):
            def weight(dst, src, signal):
                sp.dma_start(dst, src.rearrange("(c p) n -> p c n", p=P)).then_inc(signal, 16)

            def x_part(part):
                b0, b1 = X_PARTS[part]
                sp.dma_start(x_sb[:, b0:b1, :],
                             x[b0 * P:b1 * P, :].rearrange("(b p) d -> p b d", p=P)).then_inc(x_in[part], 16)

            sp.dma_start(cols_sb[:, :, :], cols).then_inc(cols_in, 16)
            x_part(0)
            weight(wq_sb[:, :, :], wq, w_in)
            weight(wk_sb[:, :, :], wk, w_in)
            x_part(1)
            weight(wv_sb[:, :, 0:D], wvT, wv_in)
            sp.dma_start(ident[:, :], eye).then_inc(ident_in, 16)
            x_part(2)
            sp.wait_ge(pads_set, 1)
            sp.dma_start(x_sb[0:LAST, NB - 1, :], x[(NB - 1) * P:N, :]).then_inc(x_in[-1], 16)
            weight(w3T_sb[:, :, :], w3T, lw_in)
            weight(u3T_sb[:, :, :], u3T, lw_in)
            sp.dma_start(rows_sb[:, :], rows.partition_broadcast(P)).then_inc(v_in, 16)
            sp.dma_start(asa_sb[:, :, :], asa.partition_broadcast(P)).then_inc(v_in, 16)

            def adj_rows(i, u, half, a):
                base = 6 * a if u == 0 else 5 * a
                if a == 0:
                    if not isinstance(i, int) or i >= 2:
                        wait_apart(sp, added, 3 * i - 3)
                        wait_apart(sp, nonzero_done, i - 1)
                elif not isinstance(i, int) or i >= 2:
                    wait(sp, p_done, (XB - 1) * (i - 1))
                    wait_apart(sp, p_end_done, i - 1)
                sp.dma_start(a_buf[u][:, 0:N], adj[bass.ds(i * P, P), :]).then_inc(adj_in[u], 16)

            def adj_last(a):
                if a == 0:
                    wait(sp, added, 3 * (NB - 2))
                    wait(sp, nonzero_done, NB - 2)
                else:
                    wait(sp, p_done, (XB - 1) * (NB - 2))
                    wait(sp, p_end_done, NB - 2)
                sp.dma_start(a_buf[0][0:LAST, 0:N], adj[(NB - 1) * P:N, :]).then_inc(adj_in[0], 16)

            adj_rows(0, 0, 0, 0)
            adj_rows(1, 1, 0, 0)
            weight(wsa_sb[:, :, 0:D], wsa, v_in)
            weight(wg_sb[:, :, 0:D], wgcn, v_in)
            with sp.Fori(1, (NB - 1) // 2, 1) as k:
                for u in range(2):
                    adj_rows(2 * k + u, u, k, 0)
            adj_last(0)
            sp.wait_ge(prep_mm, 5)
            sp.wait_ge(w_lo_set, 2)
            sp.dma_start(adjT_sb[:, :, :], adjT.rearrange("b p n -> p b n")).then_inc(adjT_in, 16)
            sp.wait_ge(w_lo_set, 2)
            sp.dma_start(w2_sb, w2.rearrange("(c p) n -> p c n", p=P)).then_inc(w2_in, 16)
            sp.wait_ge(w_lo_set, 5)
            sp.dma_start(w3_sb, w3.rearrange("(c p) n -> p c n", p=P)).then_inc(w3_in, 16)
            sp.wait_ge(exp1_done, NB)
            adj_rows(0, 0, 0, 1)
            adj_rows(1, 1, 0, 1)
            with sp.Fori(1, (NB - 1) // 2, 1) as k:
                for u in range(2):
                    adj_rows(2 * k + u, u, k, 1)
            adj_last(1)

            def send(i):
                wait(sp, x_added, NB + i + 1)
                sp.dma_start(out[bass.ds(i * P, P), :], x_sb[:, i, :]).then_inc(out_sent, 16)

            with sp.Fori(0, NB - 1, 1) as i:
                send(i)
            wait(sp, x_added, 2 * NB)
            sp.dma_start(out[(NB - 1) * P:N, :], x_sb[0:LAST, NB - 1, :]).then_inc(out_sent, 16)
            sp.wait_ge(out_sent, 16 * NB)

        @block.gpsimd
        def _(pool):
            pool.memset(x_sb[64:P, NB - 1, :], 0.0).then_inc(pads_set, 1)
            pool.wait_ge(pads_set, 1)
            pool.memset(mhalf[:, :], -0.5)
            pool.memset(p_buf[:, N:NP], 0.0).then_inc(consts_set, 1)
            pool.wait_ge(consts_set, 1)

            def ln(i, base):
                wait_apart(pool, mv_done, base + i + 1)
                pool.tensor_scalar(veps[:, :], mv[:, 1:2], EPS, None, ALU.add).then_inc(veps_set, 1)
                pool.tensor_scalar(negmean[:, :], mv[:, 0:1], -1.0, None, ALU.mult)
                wait(pool, veps_set, len(X_PARTS) + base - NB + i + 1)
                pool.tensor_tensor(mr_all[:, i, 1:2], veps[:, :], mhalf[:, :], ALU.pow).then_inc(rstd_set, 1)
                wait(pool, rstd_set, len(X_PARTS) + base - NB + i + 1)
                pool.tensor_tensor(mr_all[:, i, 0:1], negmean[:, :], mr_all[:, i, 1:2], ALU.mult).then_inc(ln_done, 1)

            start_counts(pool, ln_done, x1_added)
            for part, (b0, b1) in enumerate(X_PARTS):
                b1 = NB if part == len(X_PARTS) - 1 else b1
                wait(pool, mv_done, b1)
                pool.tensor_scalar(mr_all[:, b0:b1, 1], mr_all[:, b0:b1, 1], EPS, None, ALU.add)
                pool.tensor_scalar(mr_all[:, b0:b1, 0], mr_all[:, b0:b1, 0], -1.0, None,
                                   ALU.mult).then_inc(veps_set, 1)
                pool.wait_ge(veps_set, part + 1)
                pool.tensor_tensor(mr_all[:, b0:b1, 1], mr_all[:, b0:b1, 1], mhalf[:, 0:1].broadcast_to((P, b1 - b0)),
                                   ALU.pow).then_inc(rstd_set, 1)
                pool.wait_ge(rstd_set, part + 1)
                pool.tensor_tensor(mr_all[:, b0:b1, 0], mr_all[:, b0:b1, 0], mr_all[:, b0:b1, 1],
                                   ALU.mult).then_inc(ln_done, b1 - b0)

            def count(i, rows):
                wait(pool, counted, i + 1)
                wait(pool, nonzero_done, i + 1)
                pool.tensor_tensor(cnt[0:rows, 0:N], f(cnt[0:rows, 0:N]), f(m_tmp[0:rows, 0:N]),
                                   ALU.add).then_inc(counted, 1)

            pool.memset(f(cnt[:, :]), 0.0).then_inc(counted, 1)
            count(0, P)
            wait(pool, z_done, NB)
            pool.wait_ge(v_in, 64)
            pool.tensor_tensor(x_sb[:, :, :], x_sb[:, :, :], bv_row.unsqueeze(1).broadcast_to((P, NB, D)),
                               ALU.add).then_inc(bv_added, 1)
            with pool.Fori(0, NB - 2, 1) as i:
                count(i + 1, P)
                ln(i, NB)
            count(NB - 1, LAST)
            pool.wait_ge(counted, NB + 1)
            for i in range(NB - 2, NB):
                ln(i, NB)

            def sums(i, u, j0=0, j1=NB):
                if not isinstance(i, int) or i >= 2:
                    wait(pool, exp1_done, i - 1)
                return pool.tensor_tensor(tiles(s_pair[u][:, :])[:, j0:j1, :],
                                          slb[:, bass.ds(i * P, P)].unsqueeze(1).broadcast_to((P, j1 - j0, P)),
                                          right_all[:, j0:j1].unsqueeze(2).broadcast_to((P, j1 - j0, P)), ALU.add)

            def adj_lo(i):
                wait(pool, xb_done, i)
                wait(pool, ahi_done, i + 1)
                pool.tensor_tensor(at_lo[:, :], adjT_sb[:, i, :], f(at_hi[:, :]), ALU.subtract).then_inc(alo_done, 1)

            def add_half(i):
                wait(pool, half_done, i + 1)
                pool.tensor_tensor(x_sb[:, i, :], x_sb[:, i, :], th_buf[:, :], ALU.add).then_inc(x1_added, 1)

            adj_lo(0)
            wait(pool, vlo_done, NB + 2 * EARLY)
            sums(0, 0, 0, EARLY)
            wait(pool, vlo_done, 3 * NB)
            sums(0, 0, EARLY, NB).then_inc(sums_done, 1)
            sums(1, 1).then_inc(sums_done, 1)
            adj_lo(1)
            sums(2, 0).then_inc(sums_done, 1)

            def step1(i, u):
                inside = not isinstance(i, int)
                if inside or i + 3 < NB:
                    sums(i + 3, 1 - u).then_inc(sums_done, 1)
                if inside or i + 2 < NB:
                    adj_lo(i + 2)
                if inside or i >= 1:
                    ln(i - 1, 2 * NB)
                add_half(i)

            step1(0, 0)
            with pool.Fori(0, (NB - 5) // 2, 1) as k:
                step1(2 * k + 1, 1)
                step1(2 * k + 2, 0)
            for i in range(NB - 4, NB):
                step1(i, i % 2)
            ln(NB - 1, 2 * NB)
            with pool.Fori(0, NB, 1) as i:
                ln(i, 3 * NB)

            def plus_eye(i, u, half_i):
                wait(pool, adj_in[u], 16 * (half_i + 1 + (6 if u == 0 else 5)))
                pool.tensor_tensor(a_buf[u][:, bass.ds(i * P, P)], a_buf[u][:, bass.ds(i * P, P)], ident[:, :],
                                   ALU.add).then_inc(eye_added, 1)

            def times_s(i, u):
                for b, (at, end) in enumerate(P_CHUNKS[:-1]):
                    wait(pool, exp_done, XB * (NB + i) + b + 1)
                    pool.tensor_tensor(p_buf[:, at:end], p_buf[:, at:end], a_buf[u][:, at:end],
                                       ALU.mult).then_inc(p_done, 1)

            plus_eye(0, 0, 0)
            plus_eye(1, 1, 0)
            with pool.Fori(0, (NB - 3) // 2, 1) as k:
                for u in range(2):
                    times_s(2 * k + u, u)
                    plus_eye(2 * k + u + 2, u, k + 1)
            times_s(NB - 3, 0)
            pool.wait_ge(adj_in[0], 16 * ((NB - 1) // 2 + 1 + 6))
            pool.tensor_tensor(a_buf[0][:, (NB - 1) * P:N], a_buf[0][:, (NB - 1) * P:N], ident[:, 0:LAST],
                               ALU.add).then_inc(eye_added, 1)
            times_s(NB - 2, 1)
            times_s(NB - 1, 0)

        @block.scalar
        def _(act):
            start_counts(act, th_done, t1_done)

            def split_w(dst, src):
                act.activation(dst, src, ACT.Copy).then_inc(w_hi_set, 1)

            def h_hi_part(i, layer):
                wait(act, zt_done, layer * NB + i + 1)
                if layer in (1, 2) and i >= 3:
                    wait(act, proj_done, layer * NB + i - 2)
                act.activation(h_block(i, layer)[0], ps_x[:, i % 2, 0:D].rearrange("p (c n) -> p c n", c=C),
                               ACT.Relu).then_inc(hhi_done, 1)

            def z(i, layer):
                wait(act, ln_done, layer * NB + i + 1)
                if i >= 2:
                    wait(act, zt_done, layer * NB + i - 1)
                act.activation(z_buf[:, i % 2, :], x_sb[:, i, :], ACT.Identity, bias=mr_all[:, i, 0:1],
                               scale=mr_all[:, i, 1:2]).then_inc(z_done, 1)

            def values(i, layer):
                u, bank = i % 2, v_bank(i, layer)
                if layer == 2:
                    wait(act, biased, i + 1)
                    act.activation(v_hi[:, i, 0:D], vb_buf[:, u, :], ACT.Copy).then_inc(vhi_done, 1)
                else:
                    wait(act, proj_done, layer * NB + i + 1)
                    if layer == 1:
                        act.activation(slb[:, i * P:(i + 1) * P], ps_left[u][:, 0:P], ACT.Copy, scale=TINY)
                        act.activation(g[0][:, i, :], ps_pair[u][:, 0:W], ACT.Copy).then_inc(vhi_done, 1)
                    act.activation(v_hi[:, i, 0:D], bank[:, 0:D], ACT.Copy).then_inc(vhi_done, 1)

            def first_h(layer):
                h_hi_part(0, layer)
                z(2, layer)
                h_hi_part(1, layer)
                z(3, layer)

            def project_all(layer, others={}):
                for i in range(NB + 1):
                    if i in others:
                        others[i]()
                    if i + 2 < NB:
                        h_hi_part(i + 2, layer)
                    if i >= 1:
                        values(i - 1, layer)
                    if i + 4 < NB:
                        z(i + 4, layer)

            def t_hi_part(pair, n, a):
                wait(act, t_done, a * PAIRS + pair + 1)
                for c in range(C):
                    src = ps_t[:, c * D:c * D + n]
                    if a == 0:
                        ins = act.activation(t_hi[:, c, 0:n], src, ACT.Identity, bias=bqk[:, c:c + 1])
                    else:
                        ins = act.activation(t_hi[:, c, 0:n], src, ACT.Copy)
                ins.then_inc(thi_done, 1)

            def exp(i, u, a):
                wait(act, nb_done, a * NB + i + 1)
                wait(act, pt_done, XB * (a * NB + i))
                for b, (at, end) in enumerate(P_CHUNKS):
                    act.activation(p_buf[:, at:end], s_buf[:, at:end], ACT.Exp, bias=nb[:, 0:1],
                                   scale=1.0 if a else 2.0, accum_out=rowsum3[:, u, b:b + 1]).then_inc(exp_done, 1)

            def p_hi_part(i, a):
                for b in range(XB):
                    n = min(PER_BANK, NB - PER_BANK * b) * P
                    wait(act, pt_done, XB * (a * NB + i) + b + 1)
                    if b == 0:
                        wait(act, hi_used, a * NB + i)
                        wait(act, plo_done, XB * (a * NB + i))
                    act.activation(pt_hi[:, b * BANK:b * BANK + n], ps_x[:, b, 0:n], ACT.Copy).then_inc(phi_done, 1)

            def attention(a, after_first=None, before_last=None):
                exp(0, 0, a)
                if after_first:
                    after_first()
                with act.Fori(0, (NB - 3) // 2, 1) as k:
                    i = 2 * k
                    p_hi_part(i, a)
                    exp(i + 1, 1, a)
                    t_hi_part(k + 1, 2 * P, a)
                    p_hi_part(i + 1, a)
                    exp(i + 2, 0, a)
                p_hi_part(NB - 3, a)
                exp(NB - 2, 1, a)
                t_hi_part(PAIRS - 1, P, a)
                p_hi_part(NB - 2, a)
                if before_last:
                    before_last()
                exp(NB - 1, 0, a)
                p_hi_part(NB - 1, a)

            z(0, 0)
            z(1, 0)
            h_hi_part(0, 0)
            z(2, 0)
            h_hi_part(1, 0)
            act.wait_ge(prep_cp, 1)
            act.wait_ge(wv_in, 16)
            split_w(wb_hi[:, :, :], wv_sb[:, :, :])
            z(3, 0)

            def split_gq():
                act.wait_ge(prep_cp, 4)
                split_w(wa_hi[:, :, 0:D], gq)

            project_all(0, {2: split_gq, T_STEP + 1: lambda: t_hi_part(0, 2 * P, 0)})
            act.wait_ge(prep_mm, 4)
            act.activation(uw, ps_o[:, :].rearrange("p (c n) -> p c n", c=C), ACT.Copy).then_inc(uw_set, 1)

            def weights1():
                act.wait_ge(prep_v, 6)
                wait(act, proj_done, NB)
                act.wait_ge(t_done, PAIRS)
                split_w(wa_hi[:, :, :], wsa_sb[:, :, :])
                split_w(wb_hi[:, :, :], wg_sb[:, :, :])
                split_w(wl_hi[:, :, :], wl_sb[:, :, :])
                z(0, 1)
                z(1, 1)

            def set_gram():
                act.wait_ge(prep_mm, 5)
                act.activation(gram[:, :, :], ps_o[:, :].rearrange("p (c n) -> p c n", c=C),
                               ACT.Copy).then_inc(gram_set, 1)

            attention(0, set_gram, weights1)


            def adj_hi(i):
                wait(act, ahi_used, i)
                wait(act, alo_done, i)
                act.activation(at_hi[:, :], adjT_sb[:, i, :], ACT.Copy).then_inc(ahi_done, 1)

            def first_adj():
                act.wait_ge(adjT_in, 16)
                adj_hi(0)

            first_h(1)
            project_all(1, {2: first_adj})

            def exp1(i, u):
                wait(act, leaky_done, i + 1)
                wait(act, hi1_used, i)
                wait(act, plo1_done, i)
                act.activation(pt_hi[:, :], s_pair[u][:, :], ACT.Exp, scale=-1.0 / TINY).then_inc(phi1_done, 1)
                act.activation(p_buf[:, :], s_pair[u][:, :], ACT.Exp, scale=-1.0 / TINY).then_inc(exp1_done, 1)

            def gate_exp(i):
                wait(act, zz_done, 2 * i + 2)
                wait(act, al_set, 2 * i)
                act.activation(ez[:, :], zzb[:, :], ACT.Exp, scale=-1.0).then_inc(ez_done, 1)

            def t1(i, u):
                wait(act, sal_done, i + 1)
                wait(act, z1_done, i)
                act.activation(t1_buf[:, :], ps_xa[u][:, 0:D], ACT.Copy, scale=sal[:, 0:1]).then_inc(t1_done, 1)

            def tanh(i, u):
                wait(act, z1_done, i + 1)
                wait(act, x1_added, i)
                act.activation(th_buf[:, :], t2_buf[:, u, :], ACT.Tanh, scale=0.5).then_inc(th_done, 1)
                wait(act, th_done, i + 1)
                act.activation(th_buf[:, :], th_buf[:, :], ACT.Identity, bias=halves[:, 0:1],
                               scale=0.5).then_inc(half_done, 1)

            adj_hi(1)
            exp1(0, 0)

            def step1(i, u):
                inside = not isinstance(i, int)
                gate_exp(i)
                if inside or i + 1 < NB:
                    exp1(i + 1, 1 - u)
                t1(i, u)
                if inside or i + 2 < NB:
                    adj_hi(i + 2)
                tanh(i, u)

            step1(0, 0)
            with act.Fori(0, (NB - 3) // 2, 1) as k:
                step1(2 * k + 1, 1)
                step1(2 * k + 2, 0)
            z(0, 2)
            z(1, 2)
            step1(NB - 2, 1)
            act.wait_ge(w2_in, 16)
            wait(act, proj_done, 2 * NB)
            split_w(wa_hi[:, :, 0:D], w2_sb[:, :, :])
            first_h(2)
            step1(NB - 1, 0)

            project_all(2)
            wait(act, proj_done, 3 * NB)
            act.wait_ge(gram_set, 1)
            act.wait_ge(w3_in, 16)
            split_w(wa_hi[:, :, 0:D], gram[:, :, :])
            split_w(wb_hi[:, :, 0:D], w3_sb[:, :, :])
            z(0, 3)
            z(1, 3)
            first_h(3)
            project_all(3, {T_STEP + 1: lambda: t_hi_part(0, 2 * P, 1)})
            attention(1)

        @block.vector
        def _(dve):
            def split_w(dst, src, hi, n):
                dve.wait_ge(w_hi_set, n)
                dve.tensor_tensor(dst, src, f(hi), ALU.subtract).then_inc(w_lo_set, 1)

            def ln_stats(i, base):
                wait_apart(dve, mv_done, base + i)
                dve.bn_stats(stats[:, :], x_sb[:, i, :]).then_inc(stats_done, 1)
                wait(dve, ln_done, base + i)
                wait_apart(dve, stats_done, base + i + 1)
                dve.bn_aggr(mv[:, :], stats[:, :]).then_inc(mv_done, 1)

            def h_lo_part(i, layer):
                wait(dve, hhi_done, layer * NB + i + 1)
                hi, lo = h_block(i, layer)
                dve.scalar_tensor_tensor(out=lo, in0=ps_x[:, i % 2, 0:D].rearrange("p (c n) -> p c n", c=C),
                                         scalar=0.0, in1=f(hi), op0=ALU.max, op1=ALU.subtract).then_inc(hlo_done, 1)

            def bias(i):
                u = i % 2
                wait(dve, proj_done, 2 * NB + i + 1)
                wait(dve, vlo_done, 3 * NB + i - 1)
                dve.tensor_tensor(vb_buf[:, u, :], v_bank(i, 2)[:, 0:D], b2_row, ALU.add).then_inc(biased, 1)

            def v_lo_part(i, layer):
                u, bank = i % 2, v_bank(i, layer)
                if layer == 1:
                    wait(dve, vhi_done, NB + 2 * i + 1)
                    dve.tensor_tensor(g[1][:, i, :], ps_pair[u][:, 0:W], f(g[0][:, i, :]), ALU.subtract).then_inc(
                        vlo_done, 1)
                    wait(dve, vhi_done, NB + 2 * i + 2)
                    dve.tensor_scalar(right_all[:, bass.ds(i, 1)], bank[:, D:D + 1], TINY, None, ALU.mult)
                    dve.tensor_tensor(ext_all[:, i, :], bank[:, D + 1:D + 3], bab, ALU.add)
                    dve.tensor_tensor(v_lo[:, i, 0:D], bank[:, 0:D], f(v_hi[:, i, 0:D]),
                                      ALU.subtract).then_inc(vlo_done, 1)
                elif layer in (0, 3):
                    wait(dve, vhi_done, (4 * NB if layer else 0) + i + 1)
                    if layer == 0:
                        dve.tensor_scalar(r_all[:, i:i + 1], bank[:, D:D + 1], bqc[:, 0:1], None, ALU.add)
                    dve.tensor_tensor(v_lo[:, i, 0:D], bank[:, 0:D], f(v_hi[:, i, 0:D]),
                                      ALU.subtract).then_inc(vlo_done, 1)
                else:
                    wait(dve, vhi_done, 3 * NB + i + 1)
                    dve.tensor_tensor(v_lo[:, i, 0:D], vb_buf[:, u, :], f(v_hi[:, i, 0:D]),
                                      ALU.subtract).then_inc(vlo_done, 1)

            def first_h(layer):
                h_lo_part(0, layer)
                h_lo_part(1, layer)

            def project_all(layer, others={}):
                for i in range(NB + 1):
                    if i in others:
                        others[i]()
                    if i >= 1 and layer == 2:
                        bias(i - 1)
                    if i + 2 < NB:
                        h_lo_part(i + 2, layer)
                    if i >= 1:
                        v_lo_part(i - 1, layer)

            def t_lo_part(pair, n, a):
                wait(dve, thi_done, a * PAIRS + pair + 1)
                for c in range(C):
                    src = ps_t[:, c * D:c * D + n]
                    if a == 0:
                        ins = dve.scalar_tensor_tensor(out=t_lo[:, c, 0:n], in0=src, scalar=bqk[:, c:c + 1],
                                                       in1=f(t_hi[:, c, 0:n]), op0=ALU.add, op1=ALU.subtract)
                    else:
                        ins = dve.tensor_tensor(t_lo[:, c, 0:n], src, f(t_hi[:, c, 0:n]), ALU.subtract)
                ins.then_inc(tlo_done, 1)

            def mask_rows(i, u, half_i, a):
                if a == 0:
                    wait(dve, adj_in[u], 16 * (half_i + 1))
                    wait(dve, counted, i + 1)
                    dve.tensor_scalar(m_tmp[:, 0:N], a_buf[u][:, 0:N], 0.0, None,
                                      ALU.not_equal).then_inc(nonzero_done, 1)
                else:
                    wait(dve, eye_added, i + 1)
                    dve.tensor_scalar(m_buf[u][:, 0:N], a_buf[u][:, 0:N], 0.0, -BIG, ALU.is_le,
                                      ALU.mult).then_inc(mask3_done, 1)

            def add_adj(i, u, half_i, a):
                if a == 0:
                    wait(dve, adj_in[u], 16 * (half_i + 1))
                else:
                    wait(dve, mask3_done, i + 1)
                wait(dve, exp_done, XB * (a * NB + i))
                extra = a_buf[u] if a == 0 else m_buf[u]
                for n, (at, size) in enumerate(SCORE_CHUNKS):
                    wait_apart(dve, scored, 3 * (a * NB + i) + n + 1)
                    dve.tensor_tensor_reduce(s_buf[:, at:at + size], ps_s[:, n, 0:size],
                                             extra[:, at:at + size] if a == 0 else f(extra[:, at:at + size]),
                                             1.0, -3.4e38, ALU.add, ALU.max, mx3[:, n:n + 1]).then_inc(added, 1)
                wait(dve, added, 3 * (a * NB + i) + 3)
                dve.tensor_reduce(mx[:, :], mx3[:, 0:3], AX_X, ALU.max).then_inc(maxed, 1)
                wait(dve, maxed, a * NB + i + 1)
                if a == 0:
                    r = r_all[:, bass.ds(i, 1)]
                    dve.tensor_scalar(mr[:, :], mx[:, :], r, None, ALU.add).then_inc(shifted, 1)
                    wait(dve, shifted, i + 1)
                    dve.tensor_scalar(nb[:, :], mr[:, :], r, -2.0, ALU.subtract, ALU.mult).then_inc(nb_done, 1)
                else:
                    dve.tensor_scalar(nb[:, :], mx[:, :], -1.0, None, ALU.mult).then_inc(nb_done, 1)

            def times_s(i, u, a):
                if a:
                    at, end = P_CHUNKS[-1]
                    wait(dve, exp_done, XB * (NB + i) + XB)
                    wait(dve, eye_added, i + 1)
                    dve.tensor_tensor(p_buf[:, at:end], p_buf[:, at:end], a_buf[u][:, at:end],
                                      ALU.mult).then_inc(p_end_done, 1)

            def p_lo_part(i, a):
                for b in range(XB):
                    n = min(PER_BANK, NB - PER_BANK * b) * P
                    wait(dve, phi_done, XB * (a * NB + i) + b + 1)
                    dve.tensor_tensor(pt_lo[:, b * BANK:b * BANK + n], ps_x[:, b, 0:n],
                                      f(pt_hi[:, b * BANK:b * BANK + n]), ALU.subtract).then_inc(plo_done, 1)

            def add_out(i, u, a):
                wait(dve, exp_done, XB * (a * NB + i) + XB)
                wait(dve, rinv_done, a * NB + i)
                dve.tensor_reduce(rowsum[:, :], rowsum3[:, u, :], AX_X, ALU.add).then_inc(summed, 1)
                wait(dve, x_added, a * NB + i)
                wait(dve, summed, a * NB + i + 1)
                dve.reciprocal(rinv[:, :], rowsum[:, :]).then_inc(rinv_done, 1)
                wait(dve, rinv_done, a * NB + i + 1)
                wait(dve, agg_done, a * NB + i + 1)
                dve.scalar_tensor_tensor(out=x_sb[:, i, :], in0=ps_o[:, 0:D], scalar=rinv[:, 0:1], in1=x_sb[:, i, :],
                                         op0=ALU.mult, op1=ALU.add).then_inc(x_added, 1)
                if a == 0:
                    wait_apart(dve, x_added, i + 1)
                    ln_stats(i, NB)

            def attention(a, after_first=None, before_last=None):
                mask_rows(0, 0, 0, a)
                add_adj(0, 0, 0, a)
                mask_rows(1, 1, 0, a)
                times_s(0, 0, a)
                if after_first:
                    after_first()
                if a == 0:
                    dve.wait_ge(bv_added, 1)
                with dve.Fori(0, (NB - 3) // 2, 1) as k:
                    i = 2 * k
                    p_lo_part(i, a)
                    add_adj(i + 1, 1, k, a)
                    mask_rows(i + 2, 0, k + 1, a)
                    t_lo_part(k + 1, 2 * P, a)
                    times_s(i + 1, 1, a)
                    add_out(i, 0, a)
                    p_lo_part(i + 1, a)
                    add_adj(i + 2, 0, k + 1, a)
                    mask_rows(i + 3, 1, k + 1, a)
                    times_s(i + 2, 0, a)
                    add_out(i + 1, 1, a)
                p_lo_part(NB - 3, a)
                add_adj(NB - 2, 1, (NB - 2) // 2, a)
                mask_rows(NB - 1, 0, (NB - 1) // 2, a)
                t_lo_part(PAIRS - 1, P, a)
                times_s(NB - 2, 1, a)
                add_out(NB - 3, 0, a)
                p_lo_part(NB - 2, a)
                add_adj(NB - 1, 0, (NB - 1) // 2, a)
                times_s(NB - 1, 0, a)
                add_out(NB - 2, 1, a)
                p_lo_part(NB - 1, a)
                if before_last:
                    before_last()
                add_out(NB - 1, 0, a)

            dve.memset(f(v_hi[:, :, D:D + 1]), 1.0)
            dve.memset(f(v_hi[:, :, D + 1:W]), 0.0)
            dve.memset(f(v_lo[:, :, D:W]), 0.0)
            dve.memset(wv_sb[:, :, D + 1:W], 0.0)
            dve.memset(deg[:, :], 1.0)
            dve.memset(ones[:, :], 1.0)
            dve.memset(halves[:, :], 0.5)
            dve.wait_ge(cols_in, 16)
            for c in range(C):
                dve.tensor_copy(bq_rep[:, c, :], bq_col[:, c:c + 1].broadcast_to((P, P)))
            dve.tensor_copy(wg_sb[:, :, D:D + 1], cols_sb[:, 2, :].unsqueeze(2))
            dve.tensor_copy(wg_sb[:, :, D + 1:W], cols_sb[:, 4, :].unsqueeze(2))
            dve.tensor_copy(wsa_sb[:, :, D + 1:D + 2], cols_sb[:, 3, :].unsqueeze(2))
            dve.tensor_copy(wsa_sb[:, :, D + 2:D + 3], cols_sb[:, 5, :].unsqueeze(2))
            dve.memset(wsa_sb[:, :, D + 3:WA], 0.0).then_inc(prep_v, 1)
            start_counts(dve, rinv_done, plo_done, mv_done, vlo_done, x_added, hlo_done, t2_done, zz_done)

            def x_part_stats(part):
                b0, b1 = X_PARTS[part]
                final = part == len(X_PARTS) - 1
                b1 = NB if final else b1
                dve.wait_ge(x_in[part], 32 if final else 16)
                for i in range(b0, b1):
                    dve.bn_stats(x_stats[:, i, :], x_sb[:, i, :]).then_inc(stats_done, 1)
                for i in range(b0, b1):
                    dve.wait_ge(stats_done, i + 1)
                    dve.bn_aggr(mr_all[:, i, :], x_stats[:, i, :]).then_inc(mv_done, 1)

            x_part_stats(0)
            dve.wait_ge(prep_mm, 1)
            dve.tensor_scalar(wv_sb[:, :, D:D + 1], ps_x[:, 2, 0:C].unsqueeze(2), HALF_SCALE, None,
                              ALU.mult).then_inc(prep_cp, 1)
            first_h(0)
            dve.wait_ge(prep_mm, 2)
            dve.tensor_scalar(bqk[:, :], ps_x[:, 2, C:2 * C], HALF_SCALE, None, ALU.mult).then_inc(prep_cp, 1)
            dve.tensor_scalar(bqc[:, :], ps_x[:, 2, 2 * C:2 * C + 1], HALF_SCALE, None, ALU.mult).then_inc(prep_cp, 1)
            x_part_stats(1)
            split_w(wb_lo[:, :, :], wv_sb[:, :, :], wb_hi[:, :, :], 1)
            x_part_stats(2)

            def set_gq():
                dve.wait_ge(prep_mm, 3)
                dve.tensor_scalar(gq, ps_o[:, :].rearrange("p (c n) -> p c n", c=C), HALF_SCALE, None,
                                  ALU.mult).then_inc(prep_cp, 1)

            project_all(0, {1: set_gq, 4: lambda: split_w(wa_lo[:, :, 0:D], gq, wa_hi[:, :, 0:D], 2),
                            T_STEP + 1: lambda: t_lo_part(0, 2 * P, 0)})

            def weights1():
                dve.wait_ge(v_in, 64)
                for c in range(C):
                    for s in range(2):
                        dve.wait_ge(prep_v, 1 + 2 * c + s)
                        dve.tensor_tensor_reduce(vb_buf[:, s, :], wsa_sb[:, c, 0:D],
                                                 asa_sb[:, s, :], 1.0, 0.0, ALU.mult, ALU.add,
                                                 wlr[:, c, s:s + 1]).then_inc(prep_v, 1)
                dve.wait_ge(prep_v, 5)
                dve.tensor_copy(wl_sb[:, :, :], wlr[:, :, 0:1].broadcast_to((P, C, P)))
                dve.tensor_copy(wsa_sb[:, :, D:D + 1], wlr[:, :, 1:2]).then_inc(prep_v, 1)

            def ahead1():
                first_h(1)
                dve.wait_ge(prep_v, 6)
                split_w(wa_lo[:, :, :], wsa_sb[:, :, :], wa_hi[:, :, :], 3)
                split_w(wb_lo[:, :, :], wg_sb[:, :, :], wb_hi[:, :, :], 4)
                split_w(wl_lo[:, :, :], wl_sb[:, :, :], wl_hi[:, :, :], 5)

            attention(0, weights1, ahead1)

            project_all(1)

            def masked(i, u):
                wait(dve, sums_done, i + 1)
                dve.scalar_tensor_tensor(out=s_pair[u][:, :], in0=adjT_sb[:, i, :], scalar=0.0, in1=s_pair[u][:, :],
                                         op0=ALU.is_equal, op1=ALU.add).then_inc(masked_done, 1)

            def leaky(i, u):
                wait(dve, masked_done, i + 1)
                dve.scalar_tensor_tensor(out=s_pair[u][:, :], in0=s_pair[u][:, :], scalar=0.01, in1=s_pair[u][:, :],
                                         op0=ALU.mult, op1=ALU.max).then_inc(leaky_done, 1)

            def p1_lo(i):
                wait(dve, exp1_done, i + 1)
                wait(dve, xa_done, i)
                dve.tensor_tensor(pt_lo[:, :], p_buf[:, :], f(pt_hi[:, :]), ALU.subtract).then_inc(plo1_done, 1)

            def gates_in(i, u):
                wait(dve, xb_done, i + 1)
                wait(dve, th_done, i - 1)
                wait(dve, ez_done, i)
                dve.tensor_tensor(zz[:, :], ps_xb[u][:, D:W], ext_all[:, i, :], ALU.add).then_inc(zz_done, 1)
                dve.tensor_tensor(t2_buf[:, u, :], ps_xb[u][:, 0:D], bg_row, ALU.add).then_inc(t2_done, 1)
                wait(dve, zz_done, 2 * i + 1)
                dve.tensor_scalar(zzb[:, :], zz[:, :], -87.0, None, ALU.max).then_inc(zz_done, 1)

            def gate(i, u):
                wait(dve, xa_done, i + 1)
                wait(dve, ez_done, i + 1)
                wait(dve, ral_done, i)
                dve.tensor_scalar(al[:, 0:2], ez[:, :], 1.0, None, ALU.add).then_inc(al_set, 1)
                dve.tensor_scalar(al[:, 2:3], ps_xa[u][:, D:D + 1], EPS, None, ALU.add).then_inc(al_set, 1)
                wait(dve, al_set, 2 * i + 2)
                wait(dve, z1_done, i)
                dve.reciprocal(ral[:, :], al[:, :]).then_inc(ral_done, 1)
                wait(dve, ral_done, i + 1)
                wait(dve, t1_done, i)
                dve.tensor_tensor(sal[:, :], ral[:, 0:1], ral[:, 2:3], ALU.mult).then_inc(sal_done, 1)

            def join(i, u):
                wait(dve, t1_done, i + 1)
                wait(dve, t2_done, i + 1)
                dve.scalar_tensor_tensor(out=t2_buf[:, u, :], in0=t2_buf[:, u, :], scalar=ral[:, 1:2], in1=t1_buf[:, :],
                                         op0=ALU.mult, op1=ALU.add).then_inc(z1_done, 1)

            def stats1(i):
                wait_apart(dve, x1_added, i + 1)
                ln_stats(i, 2 * NB)

            dve.wait_ge(adjT_in, 16)
            masked(0, 0)
            leaky(0, 0)
            masked(1, 1)
            leaky(1, 1)
            p1_lo(0)

            def step1(i, u):
                inside = not isinstance(i, int)
                gates_in(i, u)
                if inside or i + 2 < NB:
                    masked(i + 2, u)
                    leaky(i + 2, u)
                gate(i, u)
                if inside or i >= 1:
                    stats1(i - 1)
                if inside or i + 1 < NB:
                    p1_lo(i + 1)
                join(i, u)

            step1(0, 0)
            with dve.Fori(0, (NB - 3) // 2, 1) as k:
                step1(2 * k + 1, 1)
                step1(2 * k + 2, 0)
            step1(NB - 2, 1)
            split_w(wa_lo[:, :, 0:D], w2_sb[:, :, :], wa_hi[:, :, 0:D], 6)
            first_h(2)
            step1(NB - 1, 0)
            stats1(NB - 1)
            dve.wait_ge(deg_mm, 1)
            dve.tensor_copy(deg[:, 0:NB - 1], ps_x[:, 2, 0:NB - 1])
            dve.tensor_copy(deg[0:LAST, NB - 1:NB], ps_x[0:LAST, 2, NB - 1:NB]).then_inc(deg_done, 1)
            dve.wait_ge(deg_done, 1)
            dve.reciprocal(rdeg[:, :], deg[:, :]).then_inc(deg_done, 1)

            project_all(2)

            def mask2(i, u):
                if not isinstance(i, int) or i >= 2:
                    wait(dve, agg2_done, i - 1)
                dve.tensor_scalar(m_buf[u][:, :], adjT_sb[:, i, :], 0.0, None, ALU.not_equal).then_inc(mask2_done, 1)

            def out2(i, u):
                wait(dve, agg2_done, i + 1)
                dve.scalar_tensor_tensor(out=x_sb[:, i, :], in0=ps_pair[u][:, 0:D], scalar=rdeg[:, bass.ds(i, 1)],
                                         in1=x_sb[:, i, :], op0=ALU.mult, op1=ALU.add).then_inc(x2_added, 1)
                wait_apart(dve, x2_added, i + 1)
                ln_stats(i, 3 * NB)

            dve.wait_ge(deg_done, 2)
            wait(dve, exp1_done, NB)
            mask2(0, 0)
            with dve.Fori(0, (NB - 1) // 2, 1) as k:
                for u in range(2):
                    mask2(2 * k + u + 1, 1 - u)
                    out2(2 * k + u, u)
            split_w(wa_lo[:, :, 0:D], gram[:, :, :], wa_hi[:, :, 0:D], 7)
            split_w(wb_lo[:, :, 0:D], w3_sb[:, :, :], wb_hi[:, :, 0:D], 8)
            first_h(3)
            out2(NB - 1, 0)

            project_all(3, {T_STEP + 1: lambda: t_lo_part(0, 2 * P, 1)})
            attention(1)

        @block.tensor
        def _(pe):
            start_counts(pe, agg_done, proj_done, agg2_done, hi_used, hi1_used, ahi_used)

            def weight_product(out_ap, lhsT, rhs):
                for m in range(C):
                    for c in range(C):
                        ins = pe.matmul(out_ap[:, m * D:(m + 1) * D], lhsT[:, c, m * P:(m + 1) * P], rhs[:, c, :],
                                        start=(c == 0), stop=(c == C - 1))
                ins.then_inc(prep_mm, 1)

            def transpose_z(i, layer):
                wait(pe, z_done, layer * NB + i + 1)
                if i >= 2:
                    wait(pe, hlo_done, layer * NB + i - 1)
                u = i % 2
                for c in range(C):
                    ins = pe.transpose(ps_x[:, u, c * P:(c + 1) * P], z_buf[:, u, c * P:(c + 1) * P], ident[:, :])
                ins.then_inc(zt_done, 1)

            def weight_column(col, w, b):
                for m in range(C):
                    for c in range(C):
                        ins = pe.matmul(ps_x[:, 2, col + m:col + m + 1], w[:, c, m * P:(m + 1) * P], b[:, c:c + 1],
                                        start=(c == 0), stop=(c == C - 1))
                return ins

            pe.wait_ge(w_in, 32)
            pe.wait_ge(prep_v, 1)
            weight_column(0, wq_sb, bk_col).then_inc(prep_mm, 1)
            pe.wait_ge(ident_in, 16)
            transpose_z(0, 0)
            transpose_z(1, 0)
            pe.wait_ge(prep_cp, 1)
            weight_column(C, wk_sb, bq_col)
            for c in range(C):
                ins = pe.matmul(ps_x[:, 2, 2 * C:2 * C + 1], bq_rep[:, c, :], bk_col[:, c:c + 1],
                                start=(c == 0), stop=(c == C - 1))
            ins.then_inc(prep_mm, 1)
            weight_product(ps_o, wq_sb, wk_sb)

            def project(i, layer):
                u, bank = i % 2, v_bank(i, layer)
                wait(pe, hlo_done, layer * NB + i + 1)
                if layer == 1 and i >= 2:
                    wait(pe, vlo_done, NB + 2 * (i - 1))
                elif layer != 1 and i >= 3:
                    wait(pe, vlo_done, {0: 0, 2: 3 * NB, 3: 4 * NB}[layer] + i - 2)
                hi, lo = h_block(i, layer)
                for c in range(C):
                    h = hi[:, c, :], lo[:, c, :]
                    wa = wa_hi[:, c, :], wa_lo[:, c, :]
                    wb = wb_hi[:, c, :], wb_lo[:, c, :]
                    a, b = (c == 0), (c == C - 1)
                    if layer == 0:
                        ins = products(pe, bank[:, 0:W], h, wb, a, b)
                    elif layer == 1:
                        products(pe, bank[:, 0:WA], h, wa, a, b)
                        products(pe, ps_pair[u][:, 0:W], h, wb, a, b)
                        ins = products(pe, ps_left[u][:, 0:P], (wl_hi[:, c, :], wl_lo[:, c, :]), h, a, b)
                    elif layer == 2:
                        ins = products(pe, bank[:, 0:D], h, [w[:, 0:D] for w in wa], a, b)
                    else:
                        ins = products(pe, bank[:, 0:D], h, [w[:, 0:D] for w in wb], a, b)
                ins.then_inc(proj_done, 1)

            def project_all(layer, weights, others={}):
                pe.wait_ge(w_lo_set, weights)
                for i in range(NB):
                    if i + 2 < NB:
                        transpose_z(i + 2, layer)
                    project(i, layer)
                    if i in others:
                        others[i]()

            def make_t(pair, at, n, a):
                wait(pe, tlo_done, a * PAIRS + pair)
                for m in range(C):
                    for c in range(C):
                        ins = products(pe, ps_t[:, m * D:m * D + n],
                                       (wa_hi[:, c, m * P:(m + 1) * P], wa_lo[:, c, m * P:(m + 1) * P]),
                                       (hT[0][:, c, bass.ds(at, n)], hT[1][:, c, bass.ds(at, n)]), c == 0, c == C - 1)
                ins.then_inc(t_done, 1)

            def score(i, u, pair, a):
                wait(pe, tlo_done, a * PAIRS + pair + 1)
                mine = slice(u * P, (u + 1) * P)
                for n, (at, size) in enumerate(SCORE_CHUNKS):
                    wait(pe, added, 3 * (a * NB + i - 1) + n + 1)
                    for c in range(C):
                        ins = products(pe, ps_s[:, n, 0:size], (t_hi[:, c, mine], t_lo[:, c, mine]),
                                       (hT[0][:, c, at:at + size], hT[1][:, c, at:at + size]), c == 0, c == C - 1)
                    ins.then_inc(scored, 1)

            def transpose_p(i, a):
                for b in range(XB):
                    if a == 0:
                        wait(pe, exp_done, XB * i + b + 1)
                    elif b < XB - 1:
                        wait(pe, p_done, (XB - 1) * i + b + 1)
                    else:
                        wait(pe, p_end_done, i + 1)
                    wait(pe, plo_done, XB * (a * NB + i - 1) + b + 1)
                    n = min(PER_BANK, NB - PER_BANK * b)
                    for t in range(n):
                        j = PER_BANK * b + t
                        ins = pe.transpose(ps_x[:, b, t * P:(t + 1) * P], p_buf[:, j * P:(j + 1) * P], ident[:, :])
                    ins.then_inc(pt_done, 1)

            def weighted(out_ap, p, v, wait_lo, hi_sem):
                for j in range(NB):
                    at = slice(j * P, (j + 1) * P)
                    pe.matmul(out_ap, p[0][:, at], v[0](j), start=(j == 0), stop=False)
                    ins = pe.matmul(out_ap, p[0][:, at], v[1](j), start=False, stop=False)
                ins.then_inc(hi_sem, 1)
                wait_lo()
                for j in range(NB):
                    ins = pe.matmul(out_ap, p[1][:, j * P:(j + 1) * P], v[0](j), start=False, stop=(j == NB - 1))
                return ins

            def aggregate(i, a, then=None):
                wait(pe, x_added, a * NB + i)
                wait(pe, phi_done, XB * (a * NB + i) + XB)

                def before_lo():
                    wait(pe, plo_done, XB * (a * NB + i) + XB)
                    if then:
                        then()

                weighted(ps_o[:, 0:D], (pt_hi, pt_lo), (lambda j: v_hi[:, j, 0:D], lambda j: v_lo[:, j, 0:D]),
                         before_lo, hi_used).then_inc(agg_done, 1)

            def attention(a, after_first=None, before_last_lo=None):
                wait(pe, vlo_done, 5 * NB if a else NB)
                score(0, 0, 0, a)
                if after_first:
                    after_first()
                transpose_p(0, a)
                if a == 0:
                    pe.wait_ge(gram_set, 1)
                with pe.Fori(0, (NB - 3) // 2, 1) as k:
                    i = 2 * k
                    score(i + 1, 1, k, a)
                    make_t(k + 1, 2 * P * (k + 1), 2 * P, a)
                    aggregate(i, a)
                    transpose_p(i + 1, a)
                    score(i + 2, 0, k + 1, a)
                    aggregate(i + 1, a)
                    transpose_p(i + 2, a)
                score(NB - 2, 1, PAIRS - 2, a)
                make_t(PAIRS - 1, (NB - 1) * P, P, a)
                aggregate(NB - 3, a)
                transpose_p(NB - 2, a)
                score(NB - 1, 0, PAIRS - 1, a)
                aggregate(NB - 2, a)
                transpose_p(NB - 1, a)
                aggregate(NB - 1, a, before_last_lo)

            def first_t(a):
                pe.wait_ge(w_lo_set, 8 if a else 2)
                make_t(0, 0, 2 * P, a)

            project_all(0, 1, {T_STEP: lambda: first_t(0)})
            pe.wait_ge(lw_in, 32)
            pe.wait_ge(prep_cp, 4)
            weight_product(ps_o, u3T_sb, w3T_sb)

            def layer3_weights():
                pe.wait_ge(uw_set, 1)
                weight_product(ps_o, w3T_sb, uw)

            def first_z(layer):
                transpose_z(0, layer)
                transpose_z(1, layer)

            attention(0, layer3_weights, lambda: first_z(1))
            wait(pe, x_added, NB)
            project_all(1, 5)

            def aggregate1(i, u):
                later = not isinstance(i, int) or i >= 2
                wait(pe, ahi_done, i + 1)
                if later:
                    wait(pe, t2_done, i - 1)
                    wait(pe, zz_done, 2 * i - 2)
                weighted(ps_xb[u][:, 0:W], (at_hi, at_lo), (lambda j: g[0][:, j, :], lambda j: g[1][:, j, :]),
                         lambda: wait(pe, alo_done, i + 1), ahi_used).then_inc(xb_done, 1)
                wait(pe, phi1_done, i + 1)
                if later:
                    wait(pe, t1_done, i - 1)
                weighted(ps_xa[u][:, 0:W], (pt_hi, pt_lo), (lambda j: v_hi[:, j, :], lambda j: v_lo[:, j, :]),
                         lambda: wait(pe, plo1_done, i + 1), hi1_used).then_inc(xa_done, 1)

            wait(pe, vlo_done, 3 * NB)
            aggregate1(0, 0)
            pe.wait_ge(counted, NB + 1)
            for j in range(NB):
                w = min(P, N - j * P)
                ins = pe.matmul(ps_x[0:w, 2, j:j + 1], f(cnt[:, j * P:j * P + w]), ones[:, :], start=True, stop=True)
            ins.then_inc(deg_mm, 1)
            aggregate1(1, 1)
            with pe.Fori(1, (NB - 1) // 2, 1) as k:
                for u in range(2):
                    aggregate1(2 * k + u, u)
            first_z(2)
            aggregate1(NB - 1, 0)

            wait(pe, t1_done, NB - 1)
            wait(pe, t2_done, NB - 1)
            project_all(2, 6)

            def aggregate2(i, u):
                wait(pe, mask2_done, i + 1)
                for j in range(NB):
                    for part in (v_hi, v_lo):
                        ins = pe.matmul(ps_pair[u][:, 0:D], m_buf[u][:, j * P:(j + 1) * P], part[:, j, 0:D],
                                        start=(j == 0 and part is v_hi), stop=(j == NB - 1 and part is v_lo))
                ins.then_inc(agg2_done, 1)

            wait(pe, vlo_done, 4 * NB)
            with pe.Fori(0, NB // 2, 1) as k:
                for u in range(2):
                    aggregate2(2 * k + u, u)
            first_z(3)
            aggregate2(NB - 1, 0)

            project_all(3, 8, {T_STEP: lambda: first_t(1)})
            attention(1)


_INS = ["x", "adj", "adjT", "wq", "wk", "wvT", "wsa", "wgcn", "w2", "w3", "w3T", "u3T", "asa", "cols", "rows", "eye"]


def kernel(**inputs):
    import numpy as _np
    import concourse.bacc as _bacc
    from concourse import mybir as _mybir
    from concourse.bass_utils import run_bass_kernel_spmd as _run

    a = {k: _np.asarray(v) for k, v in inputs.items()}
    padded = _np.zeros((NP, NP), a["adj"].dtype)
    padded[:N, :N] = a["adj"]
    adjT = padded.reshape(NB, P, NB, P).transpose(0, 3, 2, 1).reshape(NB, P, NB * P)
    laid = {
        "x": a["x"], "adj": a["adj"], "adjT": adjT,
        "wq": a["L0_gnn_Wq"], "wk": a["L0_gnn_Wk"], "wvT": a["L0_gnn_Wv"].T,
        "wsa": a["L1_gnn_W_sa"], "wgcn": a["L1_gnn_W_gcnb"], "w2": a["L2_gnn_W"],
        "w3": a["L3_gnn_W"], "w3T": a["L3_gnn_W"].T, "u3T": a["L3_gnn_U"].T,
        "asa": a["L1_gnn_a_sa"].reshape(2, D),
        "cols": _np.stack([a["L0_gnn_bq"], a["L0_gnn_bk"], a["L1_gnn_Wa"][0, :D], a["L1_gnn_Wa"][0, D:],
                           a["L1_gnn_Wb"][0, :D], a["L1_gnn_Wb"][0, D:]]).reshape(6, C, P).transpose(2, 0, 1),
        "rows": _np.concatenate([a["L0_gnn_bv"], a["L2_gnn_b"], a["L1_gnn_b_gcnb"], a["L1_gnn_ba"], a["L1_gnn_bb"]]),
        "eye": _np.eye(P, dtype=a["adj"].dtype),
    }
    nc = _bacc.Bacc("TRN2", target_bir_lowering=False, num_devices=1, dynamic_dma_scratch_size=8192)
    arrays, args = {}, []
    for name in _INS:
        v = _np.ascontiguousarray(laid[name])
        arrays[f"in_{name}_dram"] = v
        args.append(nc.dram_tensor(f"in_{name}_dram", v.shape, _mybir.dt.from_np(v.dtype), kind="ExternalInput").ap())
    args.append(nc.dram_tensor("out_dram", (N, D), _mybir.dt.float32, kind="ExternalOutput").ap())
    graph_layers_kernel(nc, *args)
    r = _run(nc, [arrays], core_ids=[0])
    return r.results[0]["out_dram"]
```

```python
from contextlib import ExitStack

import concourse.bass as bass
from concourse import mybir

ALU = mybir.AluOpType
ACT = mybir.ActivationFunctionType
F32 = mybir.dt.float32
F32R = mybir.dt.float32r
AX_X = mybir.AxisListType.X

P = 128
N = 1354
D = 256
C = D // P
NB = -(-N // P)
NP = NB * P
LAST = N - (NB - 1) * P
W = D + 2
WA = D + 4
BANK = 512
SCORE_CHUNKS = [(0, 452), (452, 452), (904, N - 904)]
PAIRS = (NB + 1) // 2
XB = 3
PER_BANK = 4
P_CHUNKS = [(b * BANK, min((b + 1) * BANK, N)) for b in range(XB)]
X_PARTS = [(0, 3), (3, 7), (7, NB - 1)]
EPS = 1e-5
BIG = 3.0e38
LEFT_STEP = 6
EARLY = NB - 3
T_STEP = 5
TINY = 2.0 ** -60
HALF_SCALE = 0.5 * D ** -0.5


def graph_layers_kernel(nc, x, adj, adjT, wq, wk, wvT, wsa, wgcn, w2, w3, w3T, u3T, asa, cols, rows, eye, out):
    with ExitStack() as ctx:
        def sb(name, shape, dt=F32):
            return ctx.enter_context(nc.sbuf_tensor(name, shape, dt))

        def ps(name, shape):
            return ctx.enter_context(nc.psum_tensor(name, shape, F32))

        def sem(name):
            return ctx.enter_context(nc.semaphore(name))

        def f(ap):
            return ap.bitcast(F32)

        def tiles(ap):
            return ap.rearrange("p (t m) -> p t m", m=P)

        x_sb = sb("x_sb", [P, NB, D])
        adjT_sb = sb("adjT_sb", [P, NB, NB * P])
        hT_hi = sb("hT_hi", [P, NB * W], F32R)
        hT_lo = sb("hT_lo", [P, NB * W], F32R)
        v_hi = sb("v_hi", [P, NB, W], F32R)
        v_lo = sb("v_lo", [P, NB, W], F32R)
        wa_hi = sb("wa_hi", [P, C, WA], F32R)
        wa_lo = sb("wa_lo", [P, C, WA], F32R)
        wb_hi = sb("wb_hi", [P, C, W], F32R)
        wb_lo = sb("wb_lo", [P, C, W], F32R)
        wv_sb = sb("wv_sb", [P, C, W])
        wsa_sb = sb("wsa_sb", [P, C, WA])
        wg_sb = sb("wg_sb", [P, C, W])
        gram = sb("gram", [P, C, D])
        x_stats = sb("x_stats", [P, NB, 6])
        asa_sb = sb("asa_sb", [P, 2, D])
        rows_sb = sb("rows_sb", [P, 3 * D + 2])
        cols_sb = sb("cols_sb", [P, 6, C])
        wlr = sb("wlr", [P, C, 2])
        bqk = sb("bqk", [P, C])
        bqc = sb("bqc", [P, 1])
        bq_rep = sb("bq_rep", [P, C, P])
        ident = sb("ident", [P, P])
        a_buf = [sb(f"a_buf{u}", [P, NP]) for u in range(2)]
        m_buf = [sb(f"m_buf{u}", [P, NP], F32R) for u in range(2)]
        s_buf = sb("s_buf", [P, NP])
        p_buf = sb("p_buf", [P, NP])
        pt_hi = sb("pt_hi", [P, NP], F32R)
        pt_lo = sb("pt_lo", [P, NP], F32R)
        at_hi = sb("at_hi", [P, NP], F32R)
        at_lo = sb("at_lo", [P, NP], F32R)
        h_hi = sb("h_hi", [P, 3, C, P], F32R)
        h_lo = sb("h_lo", [P, 3, C, P], F32R)
        z_buf = sb("z_buf", [P, 2, D])
        t1_buf = sb("t1_buf", [P, D])
        t2_buf = sb("t2_buf", [P, 2, D])
        th_buf = sb("th_buf", [P, D])
        vb_buf = sb("vb_buf", [P, 2, D])
        stats = sb("stats", [P, 6])
        mv = sb("mv", [P, 2])
        veps = sb("veps", [P, 1])
        mhalf = sb("mhalf", [P, 1])
        negmean = sb("negmean", [P, 1])
        mr_all = sb("mr_all", [P, NB, 2])
        sides = sb("sides", [P, 2, NB])
        ext_all = sb("ext_all", [P, NB, 2])
        ones = sb("ones", [P, 1])
        halves = sb("halves", [P, 1])
        r_all = sb("r_all", [P, NB])
        mx3 = sb("mx3", [P, 4])
        mx = sb("mx", [P, 1])
        mr = sb("mr", [P, 1])
        nb = sb("nb", [P, 1])
        rowsum3 = sb("rowsum3", [P, 2, XB])
        rowsum = sb("rowsum", [P, 1])
        rinv = sb("rinv", [P, 1])
        zz = sb("zz", [P, 2])
        zzb = sb("zzb", [P, 2])
        ez = sb("ez", [P, 2])
        al = sb("al", [P, 3])
        ral = sb("ral", [P, 3])
        sal = sb("sal", [P, 1])
        deg = sb("deg", [P, NB])
        rdeg = sb("rdeg", [P, NB])

        hT = [t[:, 0:C * NP].rearrange("p (c n) -> p c n", c=C) for t in (hT_hi, hT_lo)]
        g = [t[:, :].rearrange("p (b w) -> p b w", w=W) for t in (hT_hi, hT_lo)]
        slb = a_buf[0]
        s_pair = [s_buf, a_buf[1]]

        def h_block(i, layer):
            if layer in (0, 3):
                return [t[:, :, i * P:(i + 1) * P] for t in hT]
            return [t[:, i % 3, :, :] for t in (h_hi, h_lo)]

        def v_bank(i):
            return ps_s[:, i % 3, :]

        m_tmp, cnt = m_buf
        w2_sb, w3_sb = wv_sb[:, :, 0:D], wg_sb[:, :, 0:D]
        t_hi, t_lo = [h[:, 0:2, :, :].rearrange("p a c n -> p (a c n)").rearrange("p (c n) -> p c n", c=C)
                      for h in (h_hi, h_lo)]
        wq_sb, wk_sb, w3T_sb, u3T_sb, gq, uw = [
            adjT_sb[:, n // 2, (n % 2) * C * D:(n % 2 + 1) * C * D].rearrange("p (c n) -> p c n", c=C)
            for n in range(6)]
        bv_row, b2_row, bg_row, bab = rows_sb[:, 0:D], rows_sb[:, D:2 * D], rows_sb[:, 2 * D:3 * D], rows_sb[:, 3 * D:]
        bq_col, bk_col = cols_sb[:, 0, :], cols_sb[:, 1, :]

        ps_s = ps("ps_s", [P, 3, BANK])
        ps_x = ps("ps_x", [P, XB, BANK])
        ps_o = ps("ps_o", [P, BANK])
        ps_t = ps("ps_t", [P, BANK])
        ps_pair = [ps_o, ps_t]
        ps_g = [ps_t, ps_o]
        ps_xa = [ps_o[:, :], ps_s[:, 0, :]]
        ps_xb = [ps_t[:, :], ps_s[:, 1, :]]
        LEFT_BANKS = [ps_x[:, 2, :], ps_x[:, 1, :], ps_s[:, 2, :]]

        x_in = [sem(f"x_in{part}") for part in range(len(X_PARTS))]
        w_in, v_in, lw_in, adjT_in = (sem(n) for n in ("w_in", "v_in", "lw_in", "adjT_in"))
        w2_in, w3_in = sem("w2_in"), sem("w3_in")
        adj_in = [sem("adj_in0"), sem("adj_in1")]
        out_sent = sem("out_sent")
        passed = sem("passed")
        consts_set, pads_set, ident_in = sem("consts_set"), sem("pads_set"), sem("ident_in")
        prep_mm, prep_cp, prep_v = sem("prep_mm"), sem("prep_cp"), sem("prep_v")
        cols_in, wv_in, uw_set, gram_set = sem("cols_in"), sem("wv_in"), sem("uw_set"), sem("gram_set")
        w_hi_set, w_lo_set = sem("w_hi_set"), sem("w_lo_set")
        stats_done, mv_done, veps_set, ln_done = sem("stats_done"), sem("mv_done"), sem("veps_set"), sem("ln_done")
        z_done, zt_done, hhi_done, hlo_done = sem("z_done"), sem("zt_done"), sem("hhi_done"), sem("hlo_done")
        proj_done, biased = sem("proj_done"), sem("biased")
        vhi_done, vlo_done = sem("vhi_done"), sem("vlo_done")
        t_done, thi_done, tlo_done = sem("t_done"), sem("thi_done"), sem("tlo_done")
        scored, added, maxed, shifted, nb_done = (sem("scored"), sem("added"), sem("maxed"), sem("shifted"),
                                                  sem("nb_done"))
        exp_done, p_done, p_end_done, pt_done = sem("exp_done"), sem("p_done"), sem("p_end_done"), sem("pt_done")
        phi_done, plo_done, agg_done = sem("phi_done"), sem("plo_done"), sem("agg_done")
        hi_used, hi1_used, ahi_used = sem("hi_used"), sem("hi1_used"), sem("ahi_used")
        rinv_done, x_added = sem("rinv_done"), sem("x_added")
        rstd_set, early_sums = sem("rstd_set"), sem("early_sums")
        left_done, slb_set = sem("left_done"), sem("slb_set")
        bv_added, summed = sem("bv_added"), sem("summed")
        eye_added, mask3_done = sem("eye_added"), sem("mask3_done")
        sums_done, masked_done, leaky_done, exp1_done = (sem("sums_done"), sem("masked_done"), sem("leaky_done"),
                                                         sem("exp1_done"))
        nonzero_done, deg_mm = sem("nonzero_done"), sem("deg_mm")
        phi1_done, plo1_done, ahi_done, alo_done = sem("phi1_done"), sem("plo1_done"), sem("ahi_done"), sem("alo_done")
        xa_done, xb_done, t1_done = sem("xa_done"), sem("xb_done"), sem("t1_done")
        zz_done, t2_done, ez_done = sem("zz_done"), sem("t2_done"), sem("ez_done")
        al_set, ral_done, sal_done, z1_done, th_done, half_done, counted = (
            sem(n) for n in ("al_set", "ral_done", "sal_done", "z1_done", "th_done", "half_done", "counted"))
        x1_added, deg_done, mask2_done, agg2_done, x2_added = (sem("x1_added"), sem("deg_done"), sem("mask2_done"),
                                                               sem("agg2_done"), sem("x2_added"))

        from_one = [agg_done, proj_done, x1_added, agg2_done, ln_done, mv_done, th_done, vlo_done, x_added, hlo_done,
                    t1_done, t2_done, zz_done, hi_used, hi1_used, ahi_used,
                    plo_done, rinv_done]

        def start_counts(eng, *sems):
            for s in sems:
                eng.sem_inc(s, 1)

        def wait(eng, s, value):
            if not (isinstance(value, int) and value <= 0):
                eng.wait_ge(s, value + 1 if any(s is t for t in from_one) else value)

        def wait_apart(eng, s, value):
            wait(eng, s, value)
            if not isinstance(value, int):
                eng.sem_inc(passed, 1)

        def products(eng, out_ap, lhs, rhs, first, last, skip=False):
            eng.matmul(out_ap, lhs[0], rhs[0], start=first, stop=False, skip_group_check=skip)
            eng.matmul(out_ap, lhs[0], rhs[1], start=False, stop=False, skip_group_check=skip)
            return eng.matmul(out_ap, lhs[1], rhs[0], start=False, stop=last, skip_group_check=skip)

        block = ctx.enter_context(nc.Block())

        @block.sync
        def _(sp):
            def weight(dst, src, signal):
                sp.dma_start(dst, src.rearrange("(c p) n -> p c n", p=P)).then_inc(signal, 16)

            def x_part(part):
                b0, b1 = X_PARTS[part]
                sp.dma_start(x_sb[:, b0:b1, :],
                             x[b0 * P:b1 * P, :].rearrange("(b p) d -> p b d", p=P)).then_inc(x_in[part], 16)

            sp.dma_start(cols_sb[:, :, :], cols).then_inc(cols_in, 16)
            x_part(0)
            weight(wq_sb[:, :, :], wq, w_in)
            weight(wk_sb[:, :, :], wk, w_in)
            x_part(1)
            weight(wv_sb[:, :, 0:D], wvT, wv_in)
            sp.dma_start(ident[:, :], eye).then_inc(ident_in, 16)
            x_part(2)
            sp.wait_ge(pads_set, 1)
            sp.dma_start(x_sb[0:LAST, NB - 1, :], x[(NB - 1) * P:N, :]).then_inc(x_in[-1], 16)
            weight(w3T_sb[:, :, :], w3T, lw_in)
            weight(u3T_sb[:, :, :], u3T, lw_in)
            sp.dma_start(rows_sb[:, :], rows.partition_broadcast(P)).then_inc(v_in, 16)
            sp.dma_start(asa_sb[:, :, :], asa.partition_broadcast(P)).then_inc(v_in, 16)

            def adj_rows(i, u, a):
                if a == 0:
                    if not isinstance(i, int) or i >= 2:
                        wait_apart(sp, added, 3 * i - 3)
                        wait_apart(sp, nonzero_done, i - 1)
                elif not isinstance(i, int) or i >= 2:
                    wait_apart(sp, p_end_done, (XB - 1) * (i - 1))
                    wait_apart(sp, p_done, i - 1)
                sp.dma_start(a_buf[u][:, 0:N], adj[bass.ds(i * P, P), :]).then_inc(adj_in[u], 16)

            def adj_last(a):
                if a == 0:
                    wait(sp, added, 3 * (NB - 2))
                    wait(sp, nonzero_done, NB - 2)
                else:
                    wait(sp, p_done, NB - 2)
                    wait(sp, p_end_done, (XB - 1) * (NB - 2))
                sp.dma_start(a_buf[0][0:LAST, 0:N], adj[(NB - 1) * P:N, :]).then_inc(adj_in[0], 16)

            adj_rows(0, 0, 0)
            adj_rows(1, 1, 0)
            weight(wsa_sb[:, :, 0:D], wsa, v_in)
            weight(wg_sb[:, :, 0:D], wgcn, v_in)
            with sp.Fori(1, (NB - 1) // 2, 1) as k:
                for u in range(2):
                    adj_rows(2 * k + u, u, 0)
            adj_last(0)
            sp.wait_ge(prep_mm, 5)
            sp.wait_ge(w_lo_set, 2)
            sp.dma_start(adjT_sb[:, :, :], adjT.rearrange("b p n -> p b n")).then_inc(adjT_in, 16)
            sp.wait_ge(w_lo_set, 2)
            sp.dma_start(w2_sb, w2.rearrange("(c p) n -> p c n", p=P)).then_inc(w2_in, 16)
            sp.wait_ge(w_lo_set, 4)
            sp.dma_start(w3_sb, w3.rearrange("(c p) n -> p c n", p=P)).then_inc(w3_in, 16)
            sp.wait_ge(exp1_done, NB)
            adj_rows(0, 0, 1)
            adj_rows(1, 1, 1)
            with sp.Fori(1, (NB - 1) // 2, 1) as k:
                for u in range(2):
                    adj_rows(2 * k + u, u, 1)
            adj_last(1)

            def send(i):
                wait(sp, x_added, NB + i + 1)
                sp.dma_start(out[bass.ds(i * P, P), :], x_sb[:, i, :]).then_inc(out_sent, 16)

            with sp.Fori(0, NB - 1, 1) as i:
                send(i)
            wait(sp, x_added, 2 * NB)
            sp.dma_start(out[(NB - 1) * P:N, :], x_sb[0:LAST, NB - 1, :]).then_inc(out_sent, 16)
            sp.wait_ge(out_sent, 16 * NB)

        @block.gpsimd
        def _(pool):
            pool.memset(x_sb[64:P, NB - 1, :], 0.0).then_inc(pads_set, 1)
            pool.wait_ge(pads_set, 1)
            pool.memset(mhalf[:, :], -0.5)
            pool.memset(p_buf[:, N:NP], 0.0).then_inc(consts_set, 1)
            pool.wait_ge(consts_set, 1)

            def ln(i, base):
                wait_apart(pool, mv_done, base + i + 1)
                pool.tensor_scalar(veps[:, :], mv[:, 1:2], EPS, None, ALU.add).then_inc(veps_set, 1)
                pool.tensor_scalar(negmean[:, :], mv[:, 0:1], -1.0, None, ALU.mult)
                wait(pool, veps_set, len(X_PARTS) + base - NB + i + 1)
                pool.tensor_tensor(mr_all[:, i, 1:2], veps[:, :], mhalf[:, :], ALU.pow).then_inc(rstd_set, 1)
                wait(pool, rstd_set, len(X_PARTS) + base - NB + i + 1)
                pool.tensor_tensor(mr_all[:, i, 0:1], negmean[:, :], mr_all[:, i, 1:2], ALU.mult).then_inc(ln_done, 1)

            start_counts(pool, ln_done, x1_added)
            for part, (b0, b1) in enumerate(X_PARTS):
                b1 = NB if part == len(X_PARTS) - 1 else b1
                wait(pool, mv_done, b1)
                pool.tensor_scalar(mr_all[:, b0:b1, 1], mr_all[:, b0:b1, 1], EPS, None, ALU.add)
                pool.tensor_scalar(mr_all[:, b0:b1, 0], mr_all[:, b0:b1, 0], -1.0, None,
                                   ALU.mult).then_inc(veps_set, 1)
                pool.wait_ge(veps_set, part + 1)
                pool.tensor_tensor(mr_all[:, b0:b1, 1], mr_all[:, b0:b1, 1], mhalf[:, 0:1].broadcast_to((P, b1 - b0)),
                                   ALU.pow).then_inc(rstd_set, 1)
                pool.wait_ge(rstd_set, part + 1)
                pool.tensor_tensor(mr_all[:, b0:b1, 0], mr_all[:, b0:b1, 0], mr_all[:, b0:b1, 1],
                                   ALU.mult).then_inc(ln_done, b1 - b0)

            def count(i, rows):
                wait(pool, counted, i + 1)
                wait(pool, nonzero_done, i + 1)
                pool.tensor_tensor(cnt[0:rows, 0:N], f(cnt[0:rows, 0:N]), f(m_tmp[0:rows, 0:N]),
                                   ALU.add).then_inc(counted, 1)

            pool.memset(f(cnt[:, :]), 0.0).then_inc(counted, 1)
            count(0, P)
            wait(pool, z_done, NB)
            pool.wait_ge(v_in, 64)
            pool.tensor_tensor(x_sb[:, :, :], x_sb[:, :, :], bv_row.unsqueeze(1).broadcast_to((P, NB, D)),
                               ALU.add).then_inc(bv_added, 1)
            with pool.Fori(0, NB - 2, 1) as i:
                count(i + 1, P)
                ln(i, NB)
            count(NB - 1, LAST)
            pool.wait_ge(counted, NB + 1)
            for i in range(NB - 2, NB):
                ln(i, NB)

            def sums(i, u, j0=0, j1=NB):
                if not isinstance(i, int) or i >= 2:
                    wait(pool, exp1_done, i - 1)
                return pool.tensor_tensor(tiles(s_pair[u][:, :])[:, j0:j1, :],
                                          slb[:, bass.ds(i * P, P)].unsqueeze(1).broadcast_to((P, j1 - j0, P)),
                                          sides[:, 0, j0:j1].unsqueeze(2).broadcast_to((P, j1 - j0, P)), ALU.add)

            def adj_lo(i):
                wait(pool, xb_done, i)
                wait(pool, ahi_done, i + 1)
                pool.tensor_tensor(at_lo[:, :], adjT_sb[:, i, :], f(at_hi[:, :]), ALU.subtract).then_inc(alo_done, 1)

            def add_half(i):
                wait(pool, half_done, i + 1)
                pool.tensor_tensor(x_sb[:, i, :], x_sb[:, i, :], th_buf[:, :], ALU.add).then_inc(x1_added, 1)

            adj_lo(0)
            wait(pool, slb_set, 1)
            wait(pool, vlo_done, NB + 2 * EARLY)
            sums(0, 0, 0, EARLY).then_inc(early_sums, 1)
            wait(pool, vlo_done, 3 * NB)
            sums(0, 0, EARLY, NB).then_inc(sums_done, 1)
            sums(1, 1).then_inc(sums_done, 1)
            adj_lo(1)
            sums(2, 0).then_inc(sums_done, 1)

            def step1(i, u):
                inside = not isinstance(i, int)
                if inside or i + 3 < NB:
                    sums(i + 3, 1 - u).then_inc(sums_done, 1)
                if inside or i + 2 < NB:
                    adj_lo(i + 2)
                if inside or i >= 1:
                    ln(i - 1, 2 * NB)
                add_half(i)

            wait(pool, slb_set, len(LEFT_BANKS))
            step1(0, 0)
            with pool.Fori(0, (NB - 5) // 2, 1) as k:
                step1(2 * k + 1, 1)
                step1(2 * k + 2, 0)
            for i in range(NB - 4, NB):
                step1(i, i % 2)
            ln(NB - 1, 2 * NB)
            with pool.Fori(0, NB, 1) as i:
                ln(i, 3 * NB)

            def plus_eye(i, u, half_i):
                wait(pool, adj_in[u], 16 * (half_i + 1 + (6 if u == 0 else 5)))
                pool.tensor_tensor(a_buf[u][:, bass.ds(i * P, P)], a_buf[u][:, bass.ds(i * P, P)], ident[:, :],
                                   ALU.add).then_inc(eye_added, 1)

            def times_s(i, u):
                at, end = P_CHUNKS[0]
                wait(pool, exp_done, XB * (NB + i) + 1)
                pool.tensor_tensor(p_buf[:, at:end], p_buf[:, at:end], a_buf[u][:, at:end],
                                   ALU.mult).then_inc(p_done, 1)

            plus_eye(0, 0, 0)
            plus_eye(1, 1, 0)
            with pool.Fori(0, (NB - 3) // 2, 1) as k:
                for u in range(2):
                    times_s(2 * k + u, u)
                    plus_eye(2 * k + u + 2, u, k + 1)
            times_s(NB - 3, 0)
            pool.wait_ge(adj_in[0], 16 * ((NB - 1) // 2 + 1 + 6))
            pool.tensor_tensor(a_buf[0][:, (NB - 1) * P:N], a_buf[0][:, (NB - 1) * P:N], ident[:, 0:LAST],
                               ALU.add).then_inc(eye_added, 1)
            times_s(NB - 2, 1)
            times_s(NB - 1, 0)

        @block.scalar
        def _(act):
            start_counts(act, th_done, t1_done)

            def split_w(dst, src):
                act.activation(dst, src, ACT.Copy).then_inc(w_hi_set, 1)

            def h_hi_part(i, layer):
                wait(act, zt_done, layer * NB + i + 1)
                if layer in (1, 2) and i >= 3:
                    wait(act, proj_done, layer * NB + i - 2)
                act.activation(h_block(i, layer)[0], ps_x[:, i % 2, 0:D].rearrange("p (c n) -> p c n", c=C),
                               ACT.Relu).then_inc(hhi_done, 1)

            def z(i, layer):
                wait(act, ln_done, layer * NB + i + 1)
                if i >= 2:
                    wait(act, zt_done, layer * NB + i - 1)
                act.activation(z_buf[:, i % 2, :], x_sb[:, i, :], ACT.Identity, bias=mr_all[:, i, 0:1],
                               scale=mr_all[:, i, 1:2]).then_inc(z_done, 1)

            def values(i, layer):
                u, bank = i % 2, v_bank(i)
                if layer == 2:
                    wait(act, biased, i + 1)
                    act.activation(v_hi[:, i, 0:D], vb_buf[:, u, :], ACT.Copy).then_inc(vhi_done, 1)
                else:
                    wait(act, proj_done, layer * NB + i + 1)
                    if layer == 1:
                        act.activation(g[0][:, i, :], ps_g[u][:, 0:W], ACT.Copy).then_inc(vhi_done, 1)
                    act.activation(v_hi[:, i, 0:D], bank[:, 0:D], ACT.Copy).then_inc(vhi_done, 1)

            def first_h(layer):
                h_hi_part(0, layer)
                z(2, layer)
                h_hi_part(1, layer)
                z(3, layer)

            def project_all(layer, others={}):
                for i in range(NB + 1):
                    if i in others:
                        others[i]()
                    if i + 2 < NB:
                        h_hi_part(i + 2, layer)
                    if i >= 1:
                        values(i - 1, layer)
                    if i + 4 < NB:
                        z(i + 4, layer)

            def t_hi_part(pair, n, a):
                wait(act, t_done, a * PAIRS + pair + 1)
                for c in range(C):
                    src = ps_t[:, c * D:c * D + n]
                    if a == 0:
                        ins = act.activation(t_hi[:, c, 0:n], src, ACT.Identity, bias=bqk[:, c:c + 1])
                    else:
                        ins = act.activation(t_hi[:, c, 0:n], src, ACT.Copy)
                ins.then_inc(thi_done, 1)

            def exp(i, u, a):
                wait(act, nb_done, a * NB + i + 1)
                wait(act, pt_done, XB * (a * NB + i))
                for b, (at, end) in enumerate(P_CHUNKS):
                    act.activation(p_buf[:, at:end], s_buf[:, at:end], ACT.Exp, bias=nb[:, 0:1],
                                   scale=1.0 if a else 2.0, accum_out=rowsum3[:, u, b:b + 1]).then_inc(exp_done, 1)

            def p_hi_part(i, a):
                for b in range(XB):
                    n = min(PER_BANK, NB - PER_BANK * b) * P
                    wait(act, pt_done, XB * (a * NB + i) + b + 1)
                    if b == 0:
                        wait(act, hi_used, a * NB + i)
                        wait(act, plo_done, XB * (a * NB + i))
                    act.activation(pt_hi[:, b * BANK:b * BANK + n], ps_x[:, b, 0:n], ACT.Copy).then_inc(phi_done, 1)

            def attention(a, after_first=None, before_last=None):
                exp(0, 0, a)
                if after_first:
                    after_first()
                with act.Fori(0, (NB - 3) // 2, 1) as k:
                    i = 2 * k
                    p_hi_part(i, a)
                    exp(i + 1, 1, a)
                    t_hi_part(k + 1, 2 * P, a)
                    p_hi_part(i + 1, a)
                    exp(i + 2, 0, a)
                p_hi_part(NB - 3, a)
                exp(NB - 2, 1, a)
                t_hi_part(PAIRS - 1, P, a)
                p_hi_part(NB - 2, a)
                if before_last:
                    before_last()
                exp(NB - 1, 0, a)
                p_hi_part(NB - 1, a)

            z(0, 0)
            z(1, 0)
            h_hi_part(0, 0)
            z(2, 0)
            h_hi_part(1, 0)
            act.wait_ge(prep_cp, 1)
            act.wait_ge(wv_in, 16)
            split_w(wb_hi[:, :, :], wv_sb[:, :, :])
            z(3, 0)

            def split_gq():
                act.wait_ge(prep_cp, 4)
                split_w(wa_hi[:, :, 0:D], gq)

            project_all(0, {2: split_gq, T_STEP + 1: lambda: t_hi_part(0, 2 * P, 0)})
            act.wait_ge(prep_mm, 4)
            act.activation(uw, ps_o[:, :].rearrange("p (c n) -> p c n", c=C), ACT.Copy).then_inc(uw_set, 1)

            def weights1():
                act.wait_ge(prep_v, 6)
                wait(act, proj_done, NB)
                act.wait_ge(t_done, PAIRS)
                split_w(wa_hi[:, :, :], wsa_sb[:, :, :])
                split_w(wb_hi[:, :, :], wg_sb[:, :, :])
                z(0, 1)
                z(1, 1)

            def set_gram():
                act.wait_ge(prep_mm, 5)
                act.activation(gram[:, :, :], ps_o[:, :].rearrange("p (c n) -> p c n", c=C),
                               ACT.Copy).then_inc(gram_set, 1)

            attention(0, set_gram, weights1)


            def adj_hi(i):
                wait(act, ahi_used, i)
                wait(act, alo_done, i)
                act.activation(at_hi[:, :], adjT_sb[:, i, :], ACT.Copy).then_inc(ahi_done, 1)

            def first_adj():
                act.wait_ge(adjT_in, 16)
                adj_hi(0)

            def copy_left(part):
                n = min(PER_BANK, NB - PER_BANK * part) * P
                act.wait_ge(left_done, part + 1)
                act.activation(slb[:, part * BANK:part * BANK + n], LEFT_BANKS[part][:, 0:n],
                               ACT.Copy).then_inc(slb_set, 1)

            first_h(1)
            project_all(1, {2: first_adj, LEFT_STEP + 2: lambda: copy_left(0)})

            def exp1(i, u):
                wait(act, leaky_done, i + 1)
                wait(act, hi1_used, i)
                wait(act, plo1_done, i)
                act.activation(pt_hi[:, :], s_pair[u][:, :], ACT.Exp, scale=-1.0 / TINY).then_inc(phi1_done, 1)
                act.activation(p_buf[:, :], s_pair[u][:, :], ACT.Exp, scale=-1.0 / TINY).then_inc(exp1_done, 1)

            def gate_exp(i):
                wait(act, zz_done, 2 * i + 2)
                wait(act, al_set, 2 * i)
                act.activation(ez[:, :], zzb[:, :], ACT.Exp, scale=-1.0).then_inc(ez_done, 1)

            def t1(i, u):
                wait(act, sal_done, i + 1)
                wait(act, z1_done, i)
                act.activation(t1_buf[:, :], ps_xa[u][:, 0:D], ACT.Copy, scale=sal[:, 0:1]).then_inc(t1_done, 1)

            def tanh(i, u):
                wait(act, z1_done, i + 1)
                wait(act, x1_added, i)
                act.activation(th_buf[:, :], t2_buf[:, u, :], ACT.Tanh, scale=0.5).then_inc(th_done, 1)
                wait(act, th_done, i + 1)
                act.activation(th_buf[:, :], th_buf[:, :], ACT.Identity, bias=halves[:, 0:1],
                               scale=0.5).then_inc(half_done, 1)

            exp1(0, 0)
            copy_left(1)
            copy_left(2)
            adj_hi(1)

            def step1(i, u):
                inside = not isinstance(i, int)
                gate_exp(i)
                if inside or i + 1 < NB:
                    exp1(i + 1, 1 - u)
                t1(i, u)
                if inside or i + 2 < NB:
                    adj_hi(i + 2)
                tanh(i, u)

            step1(0, 0)
            with act.Fori(0, (NB - 3) // 2, 1) as k:
                step1(2 * k + 1, 1)
                step1(2 * k + 2, 0)
            z(0, 2)
            z(1, 2)
            step1(NB - 2, 1)
            act.wait_ge(w2_in, 16)
            wait(act, proj_done, 2 * NB)
            split_w(wa_hi[:, :, 0:D], w2_sb[:, :, :])
            first_h(2)
            gate_exp(NB - 1)

            project_all(2, {1: lambda: t1(NB - 1, 0), 2: lambda: tanh(NB - 1, 0)})
            wait(act, proj_done, 3 * NB)
            act.wait_ge(gram_set, 1)
            act.wait_ge(w3_in, 16)
            split_w(wa_hi[:, :, 0:D], gram[:, :, :])
            split_w(wb_hi[:, :, 0:D], w3_sb[:, :, :])
            z(0, 3)
            z(1, 3)
            first_h(3)
            project_all(3, {T_STEP + 1: lambda: t_hi_part(0, 2 * P, 1)})
            attention(1)

        @block.vector
        def _(dve):
            def split_w(dst, src, hi, n):
                dve.wait_ge(w_hi_set, n)
                dve.tensor_tensor(dst, src, f(hi), ALU.subtract).then_inc(w_lo_set, 1)

            def ln_stats(i, base):
                wait_apart(dve, mv_done, base + i)
                dve.bn_stats(stats[:, :], x_sb[:, i, :]).then_inc(stats_done, 1)
                wait(dve, ln_done, base + i)
                wait_apart(dve, stats_done, base + i + 1)
                dve.bn_aggr(mv[:, :], stats[:, :]).then_inc(mv_done, 1)

            def h_lo_part(i, layer):
                wait(dve, hhi_done, layer * NB + i + 1)
                hi, lo = h_block(i, layer)
                dve.scalar_tensor_tensor(out=lo, in0=ps_x[:, i % 2, 0:D].rearrange("p (c n) -> p c n", c=C),
                                         scalar=0.0, in1=f(hi), op0=ALU.max, op1=ALU.subtract).then_inc(hlo_done, 1)

            def bias(i):
                u = i % 2
                wait(dve, proj_done, 2 * NB + i + 1)
                wait(dve, vlo_done, 3 * NB + i - 1)
                dve.tensor_tensor(vb_buf[:, u, :], v_bank(i)[:, 0:D], b2_row, ALU.add).then_inc(biased, 1)

            def v_lo_part(i, layer):
                u, bank = i % 2, v_bank(i)
                if layer == 1:
                    wait(dve, vhi_done, NB + 2 * i + 1)
                    dve.tensor_tensor(g[1][:, i, :], ps_g[u][:, 0:W], f(g[0][:, i, :]), ALU.subtract).then_inc(
                        vlo_done, 1)
                    wait(dve, vhi_done, NB + 2 * i + 2)
                    dve.tensor_scalar(sides[:, :, i], bank[:, D:D + 2], TINY, None, ALU.mult)
                    dve.tensor_tensor(ext_all[:, i, :], bank[:, D + 2:WA], bab, ALU.add)
                    dve.tensor_tensor(v_lo[:, i, 0:D], bank[:, 0:D], f(v_hi[:, i, 0:D]),
                                      ALU.subtract).then_inc(vlo_done, 1)
                elif layer in (0, 3):
                    wait(dve, vhi_done, (4 * NB if layer else 0) + i + 1)
                    if layer == 0:
                        dve.tensor_scalar(r_all[:, i:i + 1], bank[:, D:D + 1], bqc[:, 0:1], None, ALU.add)
                    dve.tensor_tensor(v_lo[:, i, 0:D], bank[:, 0:D], f(v_hi[:, i, 0:D]),
                                      ALU.subtract).then_inc(vlo_done, 1)
                else:
                    wait(dve, vhi_done, 3 * NB + i + 1)
                    dve.tensor_tensor(v_lo[:, i, 0:D], vb_buf[:, u, :], f(v_hi[:, i, 0:D]),
                                      ALU.subtract).then_inc(vlo_done, 1)

            def first_h(layer):
                h_lo_part(0, layer)
                h_lo_part(1, layer)

            def project_all(layer, others={}):
                for i in range(NB + 1):
                    if i in others:
                        others[i]()
                    if i + 2 < NB:
                        h_lo_part(i + 2, layer)
                    if i < NB and layer == 2:
                        bias(i)
                    if i >= 1:
                        v_lo_part(i - 1, layer)

            def t_lo_part(pair, n, a):
                wait(dve, thi_done, a * PAIRS + pair + 1)
                for c in range(C):
                    src = ps_t[:, c * D:c * D + n]
                    if a == 0:
                        ins = dve.scalar_tensor_tensor(out=t_lo[:, c, 0:n], in0=src, scalar=bqk[:, c:c + 1],
                                                       in1=f(t_hi[:, c, 0:n]), op0=ALU.add, op1=ALU.subtract)
                    else:
                        ins = dve.tensor_tensor(t_lo[:, c, 0:n], src, f(t_hi[:, c, 0:n]), ALU.subtract)
                ins.then_inc(tlo_done, 1)

            def mask_rows(i, u, half_i, a):
                if a == 0:
                    wait(dve, adj_in[u], 16 * (half_i + 1))
                    wait(dve, counted, i + 1)
                    dve.tensor_scalar(m_tmp[:, 0:N], a_buf[u][:, 0:N], 0.0, None,
                                      ALU.not_equal).then_inc(nonzero_done, 1)
                else:
                    wait(dve, eye_added, i + 1)
                    dve.tensor_scalar(m_buf[u][:, 0:N], a_buf[u][:, 0:N], 0.0, -BIG, ALU.is_le,
                                      ALU.mult).then_inc(mask3_done, 1)

            def add_adj(i, u, half_i, a):
                if a == 0:
                    wait(dve, adj_in[u], 16 * (half_i + 1))
                else:
                    wait(dve, mask3_done, i + 1)
                wait(dve, exp_done, XB * (a * NB + i))
                extra = a_buf[u] if a == 0 else m_buf[u]
                for n, (at, size) in enumerate(SCORE_CHUNKS):
                    wait_apart(dve, scored, 3 * (a * NB + i) + n + 1)
                    dve.tensor_tensor_reduce(s_buf[:, at:at + size], ps_s[:, n, 0:size],
                                             extra[:, at:at + size] if a == 0 else f(extra[:, at:at + size]),
                                             1.0, -3.4e38, ALU.add, ALU.max, mx3[:, n:n + 1]).then_inc(added, 1)
                wait(dve, added, 3 * (a * NB + i) + 3)
                dve.tensor_reduce(mx[:, :], mx3[:, 0:3], AX_X, ALU.max).then_inc(maxed, 1)
                wait(dve, maxed, a * NB + i + 1)
                if a == 0:
                    r = r_all[:, bass.ds(i, 1)]
                    dve.tensor_scalar(mr[:, :], mx[:, :], r, None, ALU.add).then_inc(shifted, 1)
                    wait(dve, shifted, i + 1)
                    dve.tensor_scalar(nb[:, :], mr[:, :], r, -2.0, ALU.subtract, ALU.mult).then_inc(nb_done, 1)
                else:
                    dve.tensor_scalar(nb[:, :], mx[:, :], -1.0, None, ALU.mult).then_inc(nb_done, 1)

            def times_s(i, u, a):
                if a:
                    wait(dve, eye_added, i + 1)
                    for b, (at, end) in list(enumerate(P_CHUNKS))[1:]:
                        wait(dve, exp_done, XB * (NB + i) + b + 1)
                        dve.tensor_tensor(p_buf[:, at:end], p_buf[:, at:end], a_buf[u][:, at:end],
                                          ALU.mult).then_inc(p_end_done, 1)

            def p_lo_part(i, a):
                for b in range(XB):
                    n = min(PER_BANK, NB - PER_BANK * b) * P
                    wait(dve, phi_done, XB * (a * NB + i) + b + 1)
                    dve.tensor_tensor(pt_lo[:, b * BANK:b * BANK + n], ps_x[:, b, 0:n],
                                      f(pt_hi[:, b * BANK:b * BANK + n]), ALU.subtract).then_inc(plo_done, 1)

            def add_out(i, u, a):
                wait(dve, exp_done, XB * (a * NB + i) + XB)
                wait(dve, rinv_done, a * NB + i)
                dve.tensor_reduce(rowsum[:, :], rowsum3[:, u, :], AX_X, ALU.add).then_inc(summed, 1)
                wait(dve, x_added, a * NB + i)
                wait(dve, summed, a * NB + i + 1)
                dve.reciprocal(rinv[:, :], rowsum[:, :]).then_inc(rinv_done, 1)
                wait(dve, rinv_done, a * NB + i + 1)
                wait(dve, agg_done, a * NB + i + 1)
                dve.scalar_tensor_tensor(out=x_sb[:, i, :], in0=ps_o[:, 0:D], scalar=rinv[:, 0:1], in1=x_sb[:, i, :],
                                         op0=ALU.mult, op1=ALU.add).then_inc(x_added, 1)
                if a == 0:
                    wait_apart(dve, x_added, i + 1)
                    ln_stats(i, NB)

            def attention(a, after_first=None, before_last=None, with_last=None):
                mask_rows(0, 0, 0, a)
                add_adj(0, 0, 0, a)
                mask_rows(1, 1, 0, a)
                times_s(0, 0, a)
                if after_first:
                    after_first()
                with dve.Fori(0, (NB - 3) // 2, 1) as k:
                    i = 2 * k
                    p_lo_part(i, a)
                    add_adj(i + 1, 1, k, a)
                    mask_rows(i + 2, 0, k + 1, a)
                    t_lo_part(k + 1, 2 * P, a)
                    times_s(i + 1, 1, a)
                    if a == 0:
                        dve.wait_ge(bv_added, 1)
                    add_out(i, 0, a)
                    p_lo_part(i + 1, a)
                    add_adj(i + 2, 0, k + 1, a)
                    mask_rows(i + 3, 1, k + 1, a)
                    times_s(i + 2, 0, a)
                    add_out(i + 1, 1, a)
                p_lo_part(NB - 3, a)
                add_adj(NB - 2, 1, (NB - 2) // 2, a)
                mask_rows(NB - 1, 0, (NB - 1) // 2, a)
                t_lo_part(PAIRS - 1, P, a)
                times_s(NB - 2, 1, a)
                add_out(NB - 3, 0, a)
                p_lo_part(NB - 2, a)
                add_adj(NB - 1, 0, (NB - 1) // 2, a)
                times_s(NB - 1, 0, a)
                if before_last:
                    before_last()
                add_out(NB - 2, 1, a)
                p_lo_part(NB - 1, a)
                if with_last:
                    with_last()
                add_out(NB - 1, 0, a)

            dve.memset(f(v_hi[:, :, D:D + 1]), 1.0)
            dve.memset(f(v_hi[:, :, D + 1:W]), 0.0)
            dve.memset(f(v_lo[:, :, D:W]), 0.0)
            dve.memset(wv_sb[:, :, D + 1:W], 0.0)
            dve.memset(deg[:, :], 1.0)
            dve.memset(ones[:, :], 1.0)
            dve.memset(halves[:, :], 0.5)
            dve.wait_ge(cols_in, 16)
            for c in range(C):
                dve.tensor_copy(bq_rep[:, c, :], bq_col[:, c:c + 1].broadcast_to((P, P)))
            dve.tensor_copy(wg_sb[:, :, D:D + 1], cols_sb[:, 2, :].unsqueeze(2))
            dve.tensor_copy(wg_sb[:, :, D + 1:W], cols_sb[:, 4, :].unsqueeze(2))
            dve.tensor_copy(wsa_sb[:, :, D + 2:D + 3], cols_sb[:, 3, :].unsqueeze(2))
            dve.tensor_copy(wsa_sb[:, :, D + 3:WA], cols_sb[:, 5, :].unsqueeze(2)).then_inc(prep_v, 1)
            start_counts(dve, rinv_done, plo_done, mv_done, vlo_done, x_added, hlo_done, t2_done, zz_done)

            def x_part_stats(part):
                b0, b1 = X_PARTS[part]
                final = part == len(X_PARTS) - 1
                b1 = NB if final else b1
                dve.wait_ge(x_in[part], 32 if final else 16)
                for i in range(b0, b1):
                    dve.bn_stats(x_stats[:, i, :], x_sb[:, i, :]).then_inc(stats_done, 1)
                for i in range(b0, b1):
                    dve.wait_ge(stats_done, i + 1)
                    dve.bn_aggr(mr_all[:, i, :], x_stats[:, i, :]).then_inc(mv_done, 1)

            x_part_stats(0)
            dve.wait_ge(prep_mm, 1)
            dve.tensor_scalar(wv_sb[:, :, D:D + 1], ps_x[:, 2, 0:C].unsqueeze(2), HALF_SCALE, None,
                              ALU.mult).then_inc(prep_cp, 1)
            first_h(0)
            dve.wait_ge(prep_mm, 2)
            dve.tensor_scalar(bqk[:, :], ps_x[:, 2, C:2 * C], HALF_SCALE, None, ALU.mult).then_inc(prep_cp, 1)
            dve.tensor_scalar(bqc[:, :], ps_x[:, 2, 2 * C:2 * C + 1], HALF_SCALE, None, ALU.mult).then_inc(prep_cp, 1)
            x_part_stats(1)
            split_w(wb_lo[:, :, :], wv_sb[:, :, :], wb_hi[:, :, :], 1)
            x_part_stats(2)

            def set_gq():
                dve.wait_ge(prep_mm, 3)
                dve.tensor_scalar(gq, ps_o[:, :].rearrange("p (c n) -> p c n", c=C), HALF_SCALE, None,
                                  ALU.mult).then_inc(prep_cp, 1)

            project_all(0, {1: set_gq, 4: lambda: split_w(wa_lo[:, :, 0:D], gq, wa_hi[:, :, 0:D], 2),
                            T_STEP + 1: lambda: t_lo_part(0, 2 * P, 0)})

            def weights1():
                dve.wait_ge(v_in, 64)
                for c in range(C):
                    for s in range(2):
                        dve.wait_ge(prep_v, 1 + 2 * c + s)
                        dve.tensor_tensor_reduce(vb_buf[:, s, :], wsa_sb[:, c, 0:D],
                                                 asa_sb[:, 1 - s, :], 1.0, 0.0, ALU.mult, ALU.add,
                                                 wlr[:, c, s:s + 1]).then_inc(prep_v, 1)
                dve.wait_ge(prep_v, 5)
                dve.tensor_copy(wsa_sb[:, :, D:D + 2], wlr[:, :, :]).then_inc(prep_v, 1)

            def split_weights1():
                dve.wait_ge(prep_v, 6)
                split_w(wa_lo[:, :, :], wsa_sb[:, :, :], wa_hi[:, :, :], 3)
                split_w(wb_lo[:, :, :], wg_sb[:, :, :], wb_hi[:, :, :], 4)


            attention(0, weights1, split_weights1, lambda: first_h(1))


            def masked(i, u, j0=0, j1=NB):
                at = slice(j0 * P, j1 * P)
                if j1 < NB:
                    dve.wait_ge(early_sums, 1)
                else:
                    wait(dve, sums_done, i + 1)
                return dve.scalar_tensor_tensor(out=s_pair[u][:, at], in0=adjT_sb[:, i, at], scalar=0.0,
                                                in1=s_pair[u][:, at], op0=ALU.is_equal, op1=ALU.add)

            def masked_early():
                dve.wait_ge(adjT_in, 16)
                masked(0, 0, 0, EARLY)

            project_all(1, {NB: masked_early})

            def leaky(i, u):
                wait(dve, masked_done, i + 1)
                dve.scalar_tensor_tensor(out=s_pair[u][:, :], in0=s_pair[u][:, :], scalar=0.01, in1=s_pair[u][:, :],
                                         op0=ALU.mult, op1=ALU.max).then_inc(leaky_done, 1)

            def p1_lo(i):
                wait(dve, exp1_done, i + 1)
                wait(dve, xa_done, i)
                dve.tensor_tensor(pt_lo[:, :], p_buf[:, :], f(pt_hi[:, :]), ALU.subtract).then_inc(plo1_done, 1)

            def gates_in(i, u):
                wait(dve, xb_done, i + 1)
                wait(dve, th_done, i - 1)
                wait(dve, ez_done, i)
                dve.tensor_tensor(zz[:, :], ps_xb[u][:, D:W], ext_all[:, i, :], ALU.add).then_inc(zz_done, 1)
                dve.tensor_tensor(t2_buf[:, u, :], ps_xb[u][:, 0:D], bg_row, ALU.add).then_inc(t2_done, 1)
                wait(dve, zz_done, 2 * i + 1)
                dve.tensor_scalar(zzb[:, :], zz[:, :], -87.0, None, ALU.max).then_inc(zz_done, 1)

            def gate(i, u):
                wait(dve, xa_done, i + 1)
                wait(dve, ez_done, i + 1)
                wait(dve, ral_done, i)
                dve.tensor_scalar(al[:, 0:2], ez[:, :], 1.0, None, ALU.add).then_inc(al_set, 1)
                dve.tensor_scalar(al[:, 2:3], ps_xa[u][:, D:D + 1], EPS, None, ALU.add).then_inc(al_set, 1)
                wait(dve, al_set, 2 * i + 2)
                wait(dve, z1_done, i)
                dve.reciprocal(ral[:, :], al[:, :]).then_inc(ral_done, 1)
                wait(dve, ral_done, i + 1)
                wait(dve, t1_done, i)
                dve.tensor_tensor(sal[:, :], ral[:, 0:1], ral[:, 2:3], ALU.mult).then_inc(sal_done, 1)

            def join(i, u):
                wait(dve, t1_done, i + 1)
                wait(dve, t2_done, i + 1)
                dve.scalar_tensor_tensor(out=t2_buf[:, u, :], in0=t2_buf[:, u, :], scalar=ral[:, 1:2], in1=t1_buf[:, :],
                                         op0=ALU.mult, op1=ALU.add).then_inc(z1_done, 1)

            def stats1(i):
                wait_apart(dve, x1_added, i + 1)
                ln_stats(i, 2 * NB)

            dve.wait_ge(adjT_in, 16)
            masked(0, 0, EARLY, NB).then_inc(masked_done, 1)
            leaky(0, 0)
            masked(1, 1).then_inc(masked_done, 1)
            p1_lo(0)
            leaky(1, 1)

            def step1(i, u):
                inside = not isinstance(i, int)
                gates_in(i, u)
                if inside or i + 2 < NB:
                    masked(i + 2, u).then_inc(masked_done, 1)
                    leaky(i + 2, u)
                gate(i, u)
                if inside or i >= 1:
                    stats1(i - 1)
                if inside or i + 1 < NB:
                    p1_lo(i + 1)
                join(i, u)

            step1(0, 0)
            with dve.Fori(0, (NB - 3) // 2, 1) as k:
                step1(2 * k + 1, 1)
                step1(2 * k + 2, 0)
            step1(NB - 2, 1)
            split_w(wa_lo[:, :, 0:D], w2_sb[:, :, :], wa_hi[:, :, 0:D], 5)
            first_h(2)
            gates_in(NB - 1, 0)

            def end_gates():
                gate(NB - 1, 0)

            def degrees():
                dve.wait_ge(deg_mm, 1)
                dve.tensor_copy(deg[:, 0:NB - 1], ps_x[:, 2, 0:NB - 1])
                dve.tensor_copy(deg[0:LAST, NB - 1:NB], ps_x[0:LAST, 2, NB - 1:NB]).then_inc(deg_done, 1)
                dve.wait_ge(deg_done, 1)
                dve.reciprocal(rdeg[:, :], deg[:, :]).then_inc(deg_done, 1)

            project_all(2, {0: end_gates, 1: lambda: stats1(NB - 2), 2: lambda: join(NB - 1, 0), 4: lambda: stats1(NB - 1), 6: degrees})

            def mask2(i, u):
                if not isinstance(i, int) or i >= 2:
                    wait(dve, agg2_done, i - 1)
                dve.tensor_scalar(m_buf[u][:, :], adjT_sb[:, i, :], 0.0, None, ALU.not_equal).then_inc(mask2_done, 1)

            def out2(i, u):
                wait(dve, agg2_done, i + 1)
                dve.scalar_tensor_tensor(out=x_sb[:, i, :], in0=ps_pair[u][:, 0:D], scalar=rdeg[:, bass.ds(i, 1)],
                                         in1=x_sb[:, i, :], op0=ALU.mult, op1=ALU.add).then_inc(x2_added, 1)
                wait_apart(dve, x2_added, i + 1)
                ln_stats(i, 3 * NB)

            dve.wait_ge(deg_done, 2)
            wait(dve, exp1_done, NB)
            mask2(0, 0)
            mask2(1, 1)
            split_w(wa_lo[:, :, 0:D], gram[:, :, :], wa_hi[:, :, 0:D], 6)
            split_w(wb_lo[:, :, 0:D], w3_sb[:, :, :], wb_hi[:, :, 0:D], 7)
            with dve.Fori(0, (NB - 3) // 2, 1) as k:
                for u in range(2):
                    mask2(2 * k + u + 2, u)
                    out2(2 * k + u, u)
            mask2(NB - 1, 0)
            out2(NB - 3, 0)
            out2(NB - 2, 1)
            first_h(3)
            out2(NB - 1, 0)

            project_all(3, {T_STEP + 1: lambda: t_lo_part(0, 2 * P, 1)})
            attention(1)

        @block.tensor
        def _(pe):
            start_counts(pe, agg_done, proj_done, agg2_done, hi_used, hi1_used, ahi_used)

            def half_product(out_ap, lhsT, rhs, m):
                for c in range(C):
                    ins = pe.matmul(out_ap[:, m * D:(m + 1) * D], lhsT[:, c, m * P:(m + 1) * P], rhs[:, c, :],
                                    start=(c == 0), stop=(c == C - 1))
                return ins

            def weight_product(out_ap, lhsT, rhs):
                for m in range(C):
                    ins = half_product(out_ap, lhsT, rhs, m)
                ins.then_inc(prep_mm, 1)

            def transpose_z(i, layer):
                wait(pe, z_done, layer * NB + i + 1)
                if i >= 2:
                    wait(pe, hlo_done, layer * NB + i - 1)
                u = i % 2
                for c in range(C):
                    ins = pe.transpose(ps_x[:, u, c * P:(c + 1) * P], z_buf[:, u, c * P:(c + 1) * P], ident[:, :])
                ins.then_inc(zt_done, 1)

            def weight_column(col, w, b):
                for m in range(C):
                    for c in range(C):
                        ins = pe.matmul(ps_x[:, 2, col + m:col + m + 1], w[:, c, m * P:(m + 1) * P], b[:, c:c + 1],
                                        start=(c == 0), stop=(c == C - 1))
                return ins

            pe.wait_ge(w_in, 32)
            pe.wait_ge(prep_v, 1)
            weight_column(0, wq_sb, bk_col).then_inc(prep_mm, 1)
            pe.wait_ge(ident_in, 16)
            transpose_z(0, 0)
            transpose_z(1, 0)
            pe.wait_ge(prep_cp, 1)
            weight_column(C, wk_sb, bq_col)
            for c in range(C):
                ins = pe.matmul(ps_x[:, 2, 2 * C:2 * C + 1], bq_rep[:, c, :], bk_col[:, c:c + 1],
                                start=(c == 0), stop=(c == C - 1))
            ins.then_inc(prep_mm, 1)
            weight_product(ps_o, wq_sb, wk_sb)

            def project(i, layer):
                u, bank = i % 2, v_bank(i)
                wait(pe, hlo_done, layer * NB + i + 1)
                if layer != 1 and i >= 3:
                    wait(pe, vlo_done, {0: 0, 2: 3 * NB, 3: 4 * NB}[layer] + i - 2)
                hi, lo = h_block(i, layer)
                h, wa, wb = ([(w[0][:, c, :], w[1][:, c, :]) for c in range(C)]
                             for w in ((hi, lo), (wa_hi, wa_lo), (wb_hi, wb_lo)))

                def product(out_ap, lhs, rhs):
                    for c in range(C):
                        ins = products(pe, out_ap, lhs[c], rhs[c], c == 0, c == C - 1)
                    return ins

                if layer == 0:
                    ins = product(bank[:, 0:W], h, wb)
                elif layer == 1:
                    if i >= 2:
                        wait(pe, vlo_done, NB + 2 * (i - 2) + 1)
                    if i == 1:
                        wait(pe, x_added, NB)
                    product(ps_g[u][:, 0:W], h, wb)
                    if i >= 3:
                        wait(pe, vlo_done, NB + 2 * (i - 3) + 2)
                    ins = product(bank[:, 0:WA], h, wa)
                elif layer == 2:
                    ins = product(bank[:, 0:D], h, [(w[0][:, 0:D], w[1][:, 0:D]) for w in wa])
                else:
                    ins = product(bank[:, 0:D], h, [(w[0][:, 0:D], w[1][:, 0:D]) for w in wb])
                ins.then_inc(proj_done, 1)

            def project_all(layer, weights, others={}):
                pe.wait_ge(w_lo_set, weights)
                for i in range(NB):
                    if i + 2 < NB:
                        transpose_z(i + 2, layer)
                    project(i, layer)
                    if i in others:
                        others[i]()

            def make_t(pair, at, n, a):
                wait(pe, tlo_done, a * PAIRS + pair)
                for m in range(C):
                    for c in range(C):
                        ins = products(pe, ps_t[:, m * D:m * D + n],
                                       (wa_hi[:, c, m * P:(m + 1) * P], wa_lo[:, c, m * P:(m + 1) * P]),
                                       (hT[0][:, c, bass.ds(at, n)], hT[1][:, c, bass.ds(at, n)]), c == 0, c == C - 1)
                ins.then_inc(t_done, 1)

            def score(i, u, pair, a, first=False):
                wait(pe, tlo_done, a * PAIRS + pair + 1)
                mine = slice(u * P, (u + 1) * P)
                for n, (at, size) in enumerate(SCORE_CHUNKS):
                    if first and n == 1:
                        wait(pe, vlo_done, 5 * NB if a else NB)
                    wait(pe, added, 3 * (a * NB + i - 1) + n + 1)
                    for c in range(C):
                        ins = products(pe, ps_s[:, n, 0:size], (t_hi[:, c, mine], t_lo[:, c, mine]),
                                       (hT[0][:, c, at:at + size], hT[1][:, c, at:at + size]), c == 0, c == C - 1)
                    ins.then_inc(scored, 1)

            def transpose_p(i, a):
                for b in range(XB):
                    if a == 0:
                        wait(pe, exp_done, XB * i + b + 1)
                    elif b == 0:
                        wait(pe, p_done, i + 1)
                    else:
                        wait(pe, p_end_done, (XB - 1) * i + b)
                    wait(pe, plo_done, XB * (a * NB + i - 1) + b + 1)
                    n = min(PER_BANK, NB - PER_BANK * b)
                    for t in range(n):
                        j = PER_BANK * b + t
                        ins = pe.transpose(ps_x[:, b, t * P:(t + 1) * P], p_buf[:, j * P:(j + 1) * P], ident[:, :])
                    ins.then_inc(pt_done, 1)

            def weighted(out_ap, p, v, wait_lo, hi_sem):
                for j in range(NB):
                    at = slice(j * P, (j + 1) * P)
                    pe.matmul(out_ap, p[0][:, at], v[0](j), start=(j == 0), stop=False)
                    ins = pe.matmul(out_ap, p[0][:, at], v[1](j), start=False, stop=False)
                ins.then_inc(hi_sem, 1)
                wait_lo()
                for j in range(NB):
                    ins = pe.matmul(out_ap, p[1][:, j * P:(j + 1) * P], v[0](j), start=False, stop=(j == NB - 1))
                return ins

            def aggregate(i, a, then=None):
                wait(pe, x_added, a * NB + i)
                wait(pe, phi_done, XB * (a * NB + i) + XB)

                def before_lo():
                    wait(pe, plo_done, XB * (a * NB + i) + XB)
                    if then:
                        then()

                weighted(ps_o[:, 0:D], (pt_hi, pt_lo), (lambda j: v_hi[:, j, 0:D], lambda j: v_lo[:, j, 0:D]),
                         before_lo, hi_used).then_inc(agg_done, 1)

            def attention(a, after_first=None, before_last_lo=None):
                wait(pe, vlo_done, (5 * NB if a else NB) - 1)
                score(0, 0, 0, a, True)
                if after_first:
                    after_first()
                    transpose_p(0, a)
                    score(1, 1, 0, a)
                    pe.wait_ge(gram_set, 1)
                else:
                    score(1, 1, 0, a)
                    transpose_p(0, a)
                with pe.Fori(0, (NB - 3) // 2, 1) as k:
                    i = 2 * k
                    make_t(k + 1, 2 * P * (k + 1), 2 * P, a)
                    aggregate(i, a)
                    transpose_p(i + 1, a)
                    score(i + 2, 0, k + 1, a)
                    aggregate(i + 1, a)
                    transpose_p(i + 2, a)
                    score(i + 3, 1, k + 1, a)
                make_t(PAIRS - 1, (NB - 1) * P, P, a)
                aggregate(NB - 3, a)
                transpose_p(NB - 2, a)
                score(NB - 1, 0, PAIRS - 1, a)
                aggregate(NB - 2, a)
                transpose_p(NB - 1, a)
                aggregate(NB - 1, a, before_last_lo)

            def first_t(a):
                pe.wait_ge(w_lo_set, 7 if a else 2)
                make_t(0, 0, 2 * P, a)

            def uw_half(m):
                pe.wait_ge(lw_in, 32)
                pe.wait_ge(prep_cp, 4)
                return half_product(ps_o, u3T_sb, w3T_sb, m)

            project_all(0, 1, {T_STEP: lambda: first_t(0), T_STEP + 1: lambda: uw_half(0),
                               T_STEP + 3: lambda: uw_half(1).then_inc(prep_mm, 1)})

            def layer3_weights():
                pe.wait_ge(uw_set, 1)
                weight_product(ps_o, w3T_sb, uw)

            def first_z(layer):
                transpose_z(0, layer)
                transpose_z(1, layer)

            attention(0, layer3_weights, lambda: first_z(1))

            def lay_left(part):
                blocks = range(part * PER_BANK, min((part + 1) * PER_BANK, NB))
                wait(pe, vlo_done, NB + 2 * (blocks[-1] + 1))
                for n, j in enumerate(blocks):
                    ins = pe.transpose(LEFT_BANKS[part][:, n * P:(n + 1) * P],
                                       sides[:, 1, j:j + 1].broadcast_to((P, P)), ident[:, :])
                ins.then_inc(left_done, 1)

            project_all(1, 4, {LEFT_STEP: lambda: lay_left(0)})

            def aggregate1(i, u, between=None):
                later = not isinstance(i, int) or i >= 2
                wait(pe, ahi_done, i + 1)
                if later:
                    wait(pe, t2_done, i - 1)
                    wait(pe, zz_done, 2 * i - 2)
                weighted(ps_xb[u][:, 0:W], (at_hi, at_lo), (lambda j: g[0][:, j, :], lambda j: g[1][:, j, :]),
                         lambda: wait(pe, alo_done, i + 1), ahi_used).then_inc(xb_done, 1)
                if between:
                    between()
                wait(pe, phi1_done, i + 1)
                if later:
                    wait(pe, t1_done, i - 1)
                weighted(ps_xa[u][:, 0:W], (pt_hi, pt_lo), (lambda j: v_hi[:, j, :], lambda j: v_lo[:, j, :]),
                         lambda: wait(pe, plo1_done, i + 1), hi1_used).then_inc(xa_done, 1)

            pe.wait_ge(slb_set, 1)
            pe.wait_ge(counted, NB + 1)
            for j in range(NB):
                w = min(P, N - j * P)
                ins = pe.matmul(ps_x[0:w, 2, j:j + 1], f(cnt[:, j * P:j * P + w]), ones[:, :], start=True, stop=True)
            ins.then_inc(deg_mm, 1)
            lay_left(1)
            wait(pe, vlo_done, 3 * NB - 1)

            aggregate1(0, 0, lambda: lay_left(2))
            aggregate1(1, 1)
            with pe.Fori(1, (NB - 1) // 2, 1) as k:
                for u in range(2):
                    aggregate1(2 * k + u, u)
            first_z(2)
            aggregate1(NB - 1, 0)

            wait(pe, t1_done, NB - 1)
            wait(pe, t2_done, NB - 1)
            project_all(2, 5)

            def aggregate2(i, u):
                wait(pe, mask2_done, i + 1)
                if not isinstance(i, int) or i >= 2:
                    wait(pe, x2_added, i - 1)
                for j in range(NB):
                    for part in (v_hi, v_lo):
                        ins = pe.matmul(ps_pair[u][:, 0:D], m_buf[u][:, j * P:(j + 1) * P], part[:, j, 0:D],
                                        start=(j == 0 and part is v_hi), stop=(j == NB - 1 and part is v_lo))
                ins.then_inc(agg2_done, 1)

            wait(pe, vlo_done, 4 * NB)
            aggregate2(0, 0)
            aggregate2(1, 1)
            with pe.Fori(1, NB // 2, 1) as k:
                for u in range(2):
                    aggregate2(2 * k + u, u)
            first_z(3)
            aggregate2(NB - 1, 0)

            project_all(3, 7, {T_STEP: lambda: first_t(1)})
            attention(1)


_INS = ["x", "adj", "adjT", "wq", "wk", "wvT", "wsa", "wgcn", "w2", "w3", "w3T", "u3T", "asa", "cols", "rows", "eye"]


def kernel(**inputs):
    import numpy as _np
    import concourse.bacc as _bacc
    from concourse import mybir as _mybir
    from concourse.bass_utils import run_bass_kernel_spmd as _run

    a = {k: _np.asarray(v) for k, v in inputs.items()}
    padded = _np.zeros((NP, NP), a["adj"].dtype)
    padded[:N, :N] = a["adj"]
    adjT = padded.reshape(NB, P, NB, P).transpose(0, 3, 2, 1).reshape(NB, P, NB * P)
    laid = {
        "x": a["x"], "adj": a["adj"], "adjT": adjT,
        "wq": a["L0_gnn_Wq"], "wk": a["L0_gnn_Wk"], "wvT": a["L0_gnn_Wv"].T,
        "wsa": a["L1_gnn_W_sa"], "wgcn": a["L1_gnn_W_gcnb"], "w2": a["L2_gnn_W"],
        "w3": a["L3_gnn_W"], "w3T": a["L3_gnn_W"].T, "u3T": a["L3_gnn_U"].T,
        "asa": a["L1_gnn_a_sa"].reshape(2, D),
        "cols": _np.stack([a["L0_gnn_bq"], a["L0_gnn_bk"], a["L1_gnn_Wa"][0, :D], a["L1_gnn_Wa"][0, D:],
                           a["L1_gnn_Wb"][0, :D], a["L1_gnn_Wb"][0, D:]]).reshape(6, C, P).transpose(2, 0, 1),
        "rows": _np.concatenate([a["L0_gnn_bv"], a["L2_gnn_b"], a["L1_gnn_b_gcnb"], a["L1_gnn_ba"], a["L1_gnn_bb"]]),
        "eye": _np.eye(P, dtype=a["adj"].dtype),
    }
    nc = _bacc.Bacc("TRN2", target_bir_lowering=False, num_devices=1, dynamic_dma_scratch_size=8192)
    arrays, args = {}, []
    for name in _INS:
        v = _np.ascontiguousarray(laid[name])
        arrays[f"in_{name}_dram"] = v
        args.append(nc.dram_tensor(f"in_{name}_dram", v.shape, _mybir.dt.from_np(v.dtype), kind="ExternalInput").ap())
    args.append(nc.dram_tensor("out_dram", (N, D), _mybir.dt.float32, kind="ExternalOutput").ap())
    graph_layers_kernel(nc, *args)
    r = _run(nc, [arrays], core_ids=[0])
    return r.results[0]["out_dram"]
```
